# Optimizing a Trainium2 kernel written in Bass

```python
import numpy as np
import jax
import jax.numpy as jnp

def _softmax(x, axis=-1):
    return jax.nn.softmax(x, axis=axis)

def _gelu(x):
    return jax.nn.gelu(x, approximate=True)

def _silu(x):
    return jax.nn.silu(x)

def _sigmoid(x):
    return jax.nn.sigmoid(x)

def _layernorm(x, axis=-1, eps=1e-05):
    m = jnp.mean(x, axis=axis, keepdims=True)
    v = jnp.var(x, axis=axis, keepdims=True)
    return (x - m) / jnp.sqrt(v + eps)

def _scatter_add(tgt, idx, src, axis=0):
    return tgt.at[idx].add(src)

def _segment_sum(src, seg, n):
    return jax.ops.segment_sum(src, seg, n)
kernel_name = 'mk_flamingo_gated_d1_seqx_r8_0335cd'

def setup_inputs(seed: int=0):
    np.random.seed(seed)
    _w = jnp.asarray

    def _rec_inputs():
        import jax
        import jax.numpy as jnp
        _rk = jax.random.key(seed)
        x = 0.01048 + 0.1018 * jax.random.normal(jax.random.fold_in(_rk, 1), (4, 256, 256), jnp.float32)
        _lenS = 256 - jax.random.randint(jax.random.fold_in(_rk, 7), (4,), 0, max(1, 256 // 4) + 1, jnp.int32)
        _lenS2 = 256 - jax.random.randint(jax.random.fold_in(_rk, 8), (4,), 0, max(1, 256 // 4) + 1, jnp.int32)
        _ctx_512P = jax.random.normal(jax.random.fold_in(_rk, 11), (4, 16, 64), jnp.float32)
        _ctx_512c = jax.random.dirichlet(jax.random.fold_in(_rk, 511), 0.3 * jnp.ones((16,), jnp.float32), (4, 256))
        _ctx_512t = jnp.einsum('bsk,bkd->bsd', _ctx_512c, _ctx_512P)
        _ctx_512t = _ctx_512t * jax.lax.rsqrt(jnp.mean(jnp.square(_ctx_512t)) + 1e-12) * 0.953939
        ctx_512 = -0.000292821 + 1.00034 * (_ctx_512t + 0.3 * jax.random.normal(jax.random.fold_in(_rk, 611), (4, 256, 64), jnp.float32))
        _g = jax.random.normal(jax.random.fold_in(_rk, 9001), (2, 1), jnp.float32)
        _g = jnp.sign(_g) * jnp.maximum(jnp.abs(_g), 1.0) + (_g == 0) * 1.0
        g_xattn = _g[0]
        g_ffn = _g[1]
        return (x, ctx_512, g_xattn, g_ffn)
    x, ctx_512, g_xattn, g_ffn = _rec_inputs()

    def _L0_xattn_setup():
        import jax, jax.numpy as jnp
        import numpy as np
        LRELU_ALPHA = 0.2
        MASK_VAL = -10000000000.0
        B, N, F_IN = (4, 256, 64)
        H, F_OUT = (8, 32)
        F_HID = H * F_OUT

        def gat_layer(x, adj, W, a_self, a_neigh, b):
            feat = jnp.einsum('nf,hfo->hno', x, W)
            attn_self = jnp.einsum('hno,ho->hn', feat, a_self)
            attn_neigh = jnp.einsum('hno,ho->hn', feat, a_neigh)
            e = attn_self[:, :, None] + attn_neigh[:, None, :]
            e = jax.nn.leaky_relu(e, LRELU_ALPHA)
            e = e + MASK_VAL * (1.0 - adj)[None, :, :]
            alpha = jax.nn.softmax(e, axis=-1)
            out = jnp.einsum('hnm,hmo->hno', alpha, feat) + b[:, None, :]
            out = jnp.transpose(out, (1, 0, 2)).reshape(out.shape[1], -1)
            return jax.nn.elu(out)
        key = jax.random.key(seed)
        ks = jax.random.split(key, 10)
        feats = jax.random.normal(ks[0], (B, N, F_IN), dtype=jnp.float32)
        a = (jax.random.uniform(ks[1], (B, N, N)) < 0.01).astype(jnp.float32)
        adj = jnp.maximum(a, jnp.eye(N, dtype=jnp.float32)[None])
        s0 = 1.0 / np.sqrt(F_IN)
        s1 = 1.0 / np.sqrt(F_HID)
        return {'feats': feats, 'adj': adj, 'W0': jax.random.normal(ks[2], (H, F_IN, F_OUT), dtype=jnp.float32) * s0, 'a_self0': jax.random.normal(ks[3], (H, F_OUT), dtype=jnp.float32) * 0.1, 'a_neigh0': jax.random.normal(ks[4], (H, F_OUT), dtype=jnp.float32) * 0.1, 'b0': jnp.zeros((H, F_OUT), dtype=jnp.float32), 'W1': jax.random.normal(ks[5], (H, F_HID, F_OUT), dtype=jnp.float32) * s1, 'a_self1': jax.random.normal(ks[6], (H, F_OUT), dtype=jnp.float32) * 0.1, 'a_neigh1': jax.random.normal(ks[7], (H, F_OUT), dtype=jnp.float32) * 0.1, 'b1': jnp.zeros((H, F_OUT), dtype=jnp.float32)}
    _L0_xattn_all = _L0_xattn_setup()
    _L0_xattn_in = {k: v for k, v in _L0_xattn_all.items() if k in ('W0', 'a_self0', 'a_neigh0', 'b0', 'W1', 'a_self1', 'a_neigh1', 'b1')}
    del _L0_xattn_all

    def _L0_ffn_setup():
        import jax, jax.numpy as jnp
        import numpy as np
        E, TOPK, H, I, NSH = (8, 2, 256, 640, 2)
        B, S = (2, 128)
        key = jax.random.key(seed)
        ks = jax.random.split(key, 8)
        sc = 0.02
        return {'x': jax.random.normal(ks[0], (B, S, H), dtype=jnp.float32), 'w_router': jax.random.normal(ks[1], (E, H), dtype=jnp.float32), 'wg': jax.random.normal(ks[2], (E, I, H), dtype=jnp.float32) * sc, 'wu': jax.random.normal(ks[3], (E, I, H), dtype=jnp.float32) * sc, 'wd': jax.random.normal(ks[4], (E, H, I), dtype=jnp.float32) * sc, 'sg': jax.random.normal(ks[5], (NSH, I, H), dtype=jnp.float32) * sc, 'su': jax.random.normal(ks[6], (NSH, I, H), dtype=jnp.float32) * sc, 'sd': jax.random.normal(ks[7], (NSH, H, I), dtype=jnp.float32) * sc}
    _L0_ffn_all = _L0_ffn_setup()
    _L0_ffn_in = {k: v for k, v in _L0_ffn_all.items() if k in ('w_router', 'wg', 'wu', 'wd', 'sg', 'su', 'sd')}
    del _L0_ffn_all
    return {'x': x, 'ctx_512': ctx_512, 'g_xattn': g_xattn, 'g_ffn': g_ffn, 'L0_xattn_W0': _L0_xattn_in['W0'], 'L0_xattn_a_self0': _L0_xattn_in['a_self0'], 'L0_xattn_a_neigh0': _L0_xattn_in['a_neigh0'], 'L0_xattn_b0': _L0_xattn_in['b0'], 'L0_xattn_W1': _L0_xattn_in['W1'], 'L0_xattn_a_self1': _L0_xattn_in['a_self1'], 'L0_xattn_a_neigh1': _L0_xattn_in['a_neigh1'], 'L0_xattn_b1': _L0_xattn_in['b1'], 'L0_ffn_w_router': _L0_ffn_in['w_router'], 'L0_ffn_wg': _L0_ffn_in['wg'], 'L0_ffn_wu': _L0_ffn_in['wu'], 'L0_ffn_wd': _L0_ffn_in['wd'], 'L0_ffn_sg': _L0_ffn_in['sg'], 'L0_ffn_su': _L0_ffn_in['su'], 'L0_ffn_sd': _L0_ffn_in['sd']}

def reference(x, ctx_512, g_xattn, g_ffn, L0_xattn_W0, L0_xattn_a_self0, L0_xattn_a_neigh0, L0_xattn_b0, L0_xattn_W1, L0_xattn_a_self1, L0_xattn_a_neigh1, L0_xattn_b1, L0_ffn_w_router, L0_ffn_wg, L0_ffn_wu, L0_ffn_wd, L0_ffn_sg, L0_ffn_su, L0_ffn_sd):
    import jax
    import jax.numpy as jnp

    def _L0_xattn_ref(feats, adj, W0, a_self0, a_neigh0, b0, W1, a_self1, a_neigh1, b1):
        import jax, jax.numpy as jnp
        import numpy as np
        LRELU_ALPHA = 0.2
        MASK_VAL = -10000000000.0
        B, N, F_IN = (4, 256, 64)
        H, F_OUT = (8, 32)
        F_HID = H * F_OUT

        def gat_layer(x, adj, W, a_self, a_neigh, b):
            feat = jnp.einsum('nf,hfo->hno', x, W)
            attn_self = jnp.einsum('hno,ho->hn', feat, a_self)
            attn_neigh = jnp.einsum('hno,ho->hn', feat, a_neigh)
            e = attn_self[:, :, None] + attn_neigh[:, None, :]
            e = jax.nn.leaky_relu(e, LRELU_ALPHA)
            e = e + MASK_VAL * (1.0 - adj)[None, :, :]
            alpha = jax.nn.softmax(e, axis=-1)
            out = jnp.einsum('hnm,hmo->hno', alpha, feat) + b[:, None, :]
            out = jnp.transpose(out, (1, 0, 2)).reshape(out.shape[1], -1)
            return jax.nn.elu(out)

        def per_graph(x, a):
            h = gat_layer(x, a, W0, a_self0, a_neigh0, b0)
            return gat_layer(h, a, W1, a_self1, a_neigh1, b1)
        return jax.vmap(per_graph)(feats, adj)

    def _L0_ffn_ref(x, w_router, wg, wu, wd, sg, su, sd):
        import jax, jax.numpy as jnp
        import numpy as np
        E, TOPK, H, I, NSH = (8, 2, 256, 640, 2)
        B, S = (2, 128)
        b, s, h = x.shape
        xt = x.reshape(-1, h)
        T = xt.shape[0]
        logits = jnp.einsum('th,eh->te', xt.astype(jnp.float32), w_router.astype(jnp.float32))
        scores = jax.nn.sigmoid(logits)
        topk_w, topk_i = jax.lax.top_k(scores, TOPK)
        topk_w = topk_w / jnp.sum(topk_w, axis=-1, keepdims=True)
        comb = jnp.zeros((T, E), dtype=xt.dtype)
        comb = comb.at[jnp.arange(T)[:, None], topk_i].add(topk_w.astype(xt.dtype))
        gate = jax.nn.silu(jnp.einsum('th,eih->tei', xt, wg))
        up = jnp.einsum('th,eih->tei', xt, wu)
        expert_out = jnp.einsum('tei,ehi->teh', gate * up, wd)
        out = jnp.einsum('te,teh->th', comb, expert_out)
        sgate = jax.nn.silu(jnp.einsum('th,jih->tji', xt, sg))
        sup = jnp.einsum('th,jih->tji', xt, su)
        out = out + jnp.einsum('tji,jhi->th', sgate * sup, sd)
        return out.reshape(b, s, h)
    x = x + jnp.tanh(g_xattn[0]) * _L0_xattn_ref(ctx_512, _layernorm(x, axis=-1), L0_xattn_W0, L0_xattn_a_self0, L0_xattn_a_neigh0, L0_xattn_b0, L0_xattn_W1, L0_xattn_a_self1, L0_xattn_a_neigh1, L0_xattn_b1)
    x = x + jnp.tanh(g_ffn[0]) * _L0_ffn_ref(_layernorm(x, axis=-1), L0_ffn_w_router, L0_ffn_wg, L0_ffn_wu, L0_ffn_wd, L0_ffn_sg, L0_ffn_su, L0_ffn_sd)
    return x

_drawn_inputs = setup_inputs


def setup_inputs(seed=0):
    import zlib

    import numpy as np

    out = dict(_drawn_inputs(seed))
    spreads = {'L0_xattn_b0': (0.0, 0.1), 'L0_xattn_b1': (0.0, 0.1)}
    factors = {}
    for name, (base, spread) in spreads.items():
        noise = np.random.default_rng([zlib.crc32(name.encode()), seed]).standard_normal(out[name].shape)
        drawn = base * np.exp(spread * noise) if base else spread * noise
        out[name] = jnp.asarray(drawn.astype(out[name].dtype))
    for name, factor in factors.items():
        out[name] = (out[name] * factor).astype(out[name].dtype)
    return out
```

```python
from contextlib import ExitStack

import concourse.bass as bass
from concourse import mybir

F32 = mybir.dt.float32
BF16 = mybir.dt.bfloat16
U32 = mybir.dt.uint32
I32 = mybir.dt.int32
ALU = mybir.AluOpType
ACT = mybir.ActivationFunctionType
AX = mybir.AxisListType

P = 128
B, N, D = 4, 256, 256
F_IN = 64
HEADS, FO = 8, 32
E, NSH, I = 8, 2, 640
T = B * N
HV = N // P
TT = T // P
KC = D // P
IC = I // P
TOPK = 2
SLOT_TILES = TOPK * TT + E - 1
ROW = D + 8
W_COL, ID_COL = D, D + 1
QUAD = 4
UNITS = HV * HEADS // QUAD
LAYERS = 2
LEAK = 0.2
MASK = 1e10
EPS = 1e-5
BIG = 3.0e38
GU = 2 * I
W_EXP = KC * GU + IC * D
GATE_CHUNKS = ((0, 256), (256, 256), (512, 128))
FEATX = FO + 1
PARTS = 3
FREE = 1
DSTEP_GRAPH = 32


def build(nc, x, ctx_t, w0, w1, a_self0, a_neigh0, b0, a_self1, a_neigh1, b1, g_xattn, g_ffn,
          w_router, w_experts, slots, out):
    with ExitStack() as stack:
        def sb(name, shape, dt=F32):
            return stack.enter_context(nc.sbuf_tensor(name, shape, dt))[(slice(None),) * len(shape)]

        def bank(name, shape, dt=F32):
            return stack.enter_context(nc.psum_tensor(name, shape, dt))[(slice(None),) * len(shape)]

        def sem(name):
            return stack.enter_context(nc.semaphore(name))

        weights = sb("weights", [P, (E + NSH) * W_EXP])
        rows1 = sb("rows1", [P, TT, ROW])
        rows2 = sb("rows2", [P, TT, ROW])
        ident = sb("ident", [P, P])
        ident_bf = sb("ident_bf", [P, P], BF16)
        router_w = sb("router_w", [P, KC, E])
        router_exp = sb("router_exp", [P, TT, E])
        gates = sb("gates", [P, 2])
        tanh_gates = sb("tanh_gates", [P, 2])
        hid = sb("hid", [P, 2, I])
        hid_t = sb("hid_t", [P, 2, IC, P])
        gate_tanh = sb("gate_tanh", [P, 2, 256])
        gate_silu = sb("gate_silu", [P, 2, 256])
        y_sb = sb("y_sb", [P, 2, D])
        tile_in = sb("tile_in", [P, 3, ROW])
        tile_t = sb("tile_t", [P, 2, KC, P])
        x_norm_t = sb("x_norm_t", [P, HV, KC, P])

        w1_sb = sb("w1_sb", [P, KC, D])
        a_sb = sb("a_sb", [P, LAYERS, 2 * D])

        LATE = 3
        scratch_at = [(E - LATE) * W_EXP]

        def carve(shape, dt=F32):
            n = 1
            for s in shape[1:]:
                n *= s
            n = n if dt == F32 else (n + 1) // 2
            a = scratch_at[0]
            scratch_at[0] = a + n
            assert scratch_at[0] <= E * W_EXP
            v = weights[:, a:a + n]
            if dt != F32:
                v = v.bitcast(dt)
            if len(shape) == 3:
                v = v.rearrange("p (a b) -> p a b", a=shape[1])
            if len(shape) == 4:
                v = v.rearrange("p (a b c) -> p a b c", a=shape[1], b=shape[2])
            return v

        x_in = carve([P, HV, D])
        x_norm = carve([P, HV, D])
        mask = carve([P, HV, D])
        ctx_sb = carve([P, N])
        w0_sb = carve([P, D])
        bias_sb = carve([P, LAYERS, D])
        delta = carve([P, HEADS, N], BF16)
        featx = carve([P, HV, HEADS * FEATX])
        score = carve([P, HV, 2 * HEADS])
        rest = carve([P, HV, 2 * HEADS])
        parts = carve([P, HV, 64], BF16)
        parts_t = carve([P, 2, N], BF16)
        logits = carve([P, 2, QUAD * N])
        probs_t = carve([P, 2, QUAD * HV * P])
        neg_max = carve([P, 2, QUAD])
        stats = carve([P, HV, 8])
        o_inv = carve([P, HV, HEADS])
        att = carve([P, HV, D])
        att_min = carve([P, HV, D])
        h0 = carve([P, HV, D])
        h0_t = carve([P, KC, N])
        x1 = carve([P, HV, D])
        prod = logits

        ps_z = bank("ps_z", [P, QUAD * N])
        ps_pt = bank("ps_pt", [P, QUAD * HV * P])
        ps_feat = bank("ps_feat", [P, 512])
        ps_o = bank("ps_o", [P, HV, 512])
        ps_tr = bank("ps_tr", [P, 512])
        ps_gu = ps_z
        ps_ht = ps_pt
        ps_y = ps_feat

        ld_x, ld_ctx, ld_w, ld_small = sem("ld_x"), sem("ld_ctx"), sem("ld_w"), sem("ld_small")
        ld_shared = sem("ld_shared")
        ld_expert = [sem(f"ld_expert{e}") for e in range(E)]
        const_step, const_ready, const_bf = sem("const_step"), sem("const_ready"), sem("const_bf")
        gates_ready = sem("gates_ready")
        dstep = sem("dstep")
        mask_ready, bn_ready = sem("mask_ready"), sem("bn_ready")
        dve_passed, pe_passed, pool_passed = sem("dve_passed"), sem("pe_passed"), sem("pool_passed")
        bent_ready = sem("bent_ready")
        var_ready, inv_ready = sem("var_ready"), sem("inv_ready")
        feat_ready, feat_copied, prod_ready = sem("feat_ready"), sem("feat_copied"), sem("prod_ready")
        parts_ready, parts_turned, parts_copied = sem("parts_ready"), sem("parts_turned"), sem("parts_copied")
        z_ready, z_copied, max_ready = sem("z_ready"), sem("z_copied"), sem("max_ready")
        probs_ready, probs_turned, probs_copied = sem("probs_ready"), sem("probs_turned"), sem("probs_copied")
        o_ready, min_ready, exp_ready = sem("o_ready"), sem("min_ready"), sem("exp_ready")
        h0_ready, h0_turned, h0_copied = sem("h0_ready"), sem("h0_turned"), sem("h0_copied")
        x_norm_ready, x_norm_turned, x_norm_copied = sem("x_norm_ready"), sem("x_norm_turned"), sem("x_norm_copied")
        rows_ready, router_ready, router_exped = sem("rows_ready"), sem("router_ready"), sem("router_exped")

        gu_ready, tanh_ready, silu_ready, hid_ready = sem("gu_ready"), sem("tanh_ready"), sem("silu_ready"), sem("hid_ready")
        hid_turned, hid_copied = sem("hid_turned"), sem("hid_copied")
        y_ready, y_saved, st_base = sem("y_ready"), sem("y_saved"), sem("st_base")
        r_gu, r_tanh, r_silu, r_hid = sem("r_gu"), sem("r_tanh"), sem("r_silu"), sem("r_hid")
        r_ht, r_htc, r_y, r_ysb = sem("r_ht"), sem("r_htc"), sem("r_y"), sem("r_ysb")
        r_ld = [sem(f"r_ld{i}") for i in range(3)]
        r_xt, r_xtc, r_add = sem("r_xt"), sem("r_xtc"), sem("r_add")
        fill_step, st_fill, st_rows = sem("fill_step"), sem("st_fill"), sem("st_rows")
        rt_step, rt_mm, rt_done = sem("rt_step"), sem("rt_mm"), sem("rt_done")

        w_exp = weights[:, :].rearrange("p (e w) -> p e w", e=E + NSH)

        score_r = sb("score_r", [P, TT, E])
        sel = sb("sel", [P, TOPK, TT * E])
        both_bf = sb("both_bf", [P, TT * E], BF16)
        tmp_r = sb("tmp_r", [P, TT * E])
        best = sb("best", [P, TOPK, TT])
        top_r = sb("top_r", [P, TT])
        counts = sb("counts", [P, 2, TT * E])
        tiles_r = sb("tiles_r", [P, 2, E])
        cmp_r = sb("cmp_r", [P, SLOT_TILES * E])
        pos_f = sb("pos_f", [P, TOPK, TT])
        pos = sb("pos", [P, TOPK, TT], U32)
        ramp_pri = sb("ramp_pri", [P, E])
        ramp_128 = sb("ramp_128", [P, TT])
        ramp_tile = sb("ramp_tile", [P, SLOT_TILES])
        below = sb("below", [P, P], BF16)
        ones_bf = sb("ones_bf", [P, P], BF16)
        expert_f = sb("expert_f", [P, SLOT_TILES])
        expert_i = sb("expert_i", [P, SLOT_TILES], I32)
        token_id = sb("token_id", [P, TT], I32)
        pad_row = sb("pad_row", [P, ROW])
        minus_half = sb("minus_half", [P, HV])
        zero_row = sb("zero_row", [P, D])

        out_rows = out
        block = stack.enter_context(nc.Block())

        def bcast_row(ap):
            return ap.rearrange("(o d) -> o d", o=1).to_broadcast([P, ap.shape[0]])

        @block.sync
        def _(sp):
            for dst, src in ((w0_sb[0:F_IN, :], w0), (w1_sb, w1.rearrange("(k p) n -> p k n", p=P)),
                             (router_w[:, :, :], w_router.rearrange("(k p) e -> p k e", p=P))):
                sp.dma_start(dst, src).then_inc(ld_w, 16)
            for dst, src in ((a_sb[:, 0, 0:D], a_self0), (a_sb[:, 0, D:2 * D], a_neigh0),
                             (a_sb[:, 1, 0:D], a_self1), (a_sb[:, 1, D:2 * D], a_neigh1),
                             (bias_sb[:, 0, :], b0), (bias_sb[:, 1, :], b1),
                             (gates[:, 0:1], g_xattn), (gates[:, 1:2], g_ffn)):
                sp.dma_start(dst, bcast_row(src)).then_inc(ld_small, 16)
            sp.dma_start(w_exp[:, E:E + NSH, :], w_experts[E:E + NSH].rearrange("e p w -> p e w")).then_inc(ld_shared, 16)
            for e in range(E - LATE):
                sp.dma_start(w_exp[:, e, :], w_experts[e]).then_inc(ld_expert[e], 16)
            sp.wait_ge(fill_step, 3)
            for j in range(SLOT_TILES):
                sp.dma_start(slots[j * P:(j + 1) * P, :], pad_row[:, :]).then_inc(st_fill, 16)
            sp.dma_start(out_rows[T:T + P, :], zero_row[:, :]).then_inc(st_fill, 16)
            sp.wait_ge(y_saved, TT)
            sp.wait_ge(rows_ready, TT + FREE)
            for e in range(E - LATE, E):
                sp.dma_start(w_exp[:, e, :], w_experts[e]).then_inc(ld_expert[e], 16)
            sp.wait_ge(st_rows, 16 * TOPK * TT)

            def load_tile(j, slot):
                sp.dma_start(tile_in[:, slot, :], slots[bass.ds(j * P, P), :]).then_inc(r_ld[slot], 16)

            for j in range(3):
                load_tile(j, j)
            FULL = (SLOT_TILES - 3) // 3
            with sp.Fori(0, FULL) as q:
                for s in range(3):
                    sp.wait_ge(r_add, 16 * (3 * q + s + 1))
                    load_tile(3 * q + 3 + s, s)
            for j in range(3 + 3 * FULL, SLOT_TILES):
                sp.wait_ge(r_add, 16 * (j - 2))
                load_tile(j, j % 3)
            sp.wait_ge(r_add, 16 * SLOT_TILES)

        @block.gpsimd
        def _(pool):
            pool.sem_inc(rows_ready, FREE)
            pool.memset(ident[:, :], 0.0).then_inc(const_step, 1)
            pool.memset(delta, 0.0).then_inc(const_step, 1)
            pool.memset(parts, 0.0).then_inc(const_step, 1)
            pool.memset(featx, 1.0).then_inc(const_step, 1)
            pool.memset(minus_half[:, :], -0.5).then_inc(const_step, 1)
            pool.memset(ones_bf[:, :], 1.0).then_inc(const_step, 1)
            pool.memset(below[:, :], 1.0).then_inc(const_step, 1)
            pool.wait_ge(const_step, 7)
            pool.affine_select(out=ident[:, :], in_=ident[:, :], compare_op=ALU.not_equal, fill=1.0, base=0,
                               pattern=[[-1, P]], channel_multiplier=1).then_inc(const_step, 1)
            pool.affine_select(out=below[:, :], in_=below[:, :], compare_op=ALU.is_gt, fill=0.0, base=0,
                               pattern=[[1, P]], channel_multiplier=-1).then_inc(const_step, 1)
            n = 9
            for part in range(PARTS):
                pool.wait_ge(const_step, n)
                pool.affine_select(out=delta, in_=delta, compare_op=ALU.not_equal, fill=1.0,
                                   base=-part * HEADS, pattern=[[-1, HEADS], [0, N]],
                                   channel_multiplier=1).then_inc(const_step, 1)
                n += 1
            pool.wait_ge(const_step, n)
            pool.tensor_copy(ident_bf[:, :], ident[:, :]).then_inc(const_ready, 1)
            pool.iota(ramp_pri[:, :], pattern=[[-1, E]], base=E, channel_multiplier=0,
                      allow_small_or_imprecise_dtypes=True).then_inc(const_bf, 1)
            pool.iota(ramp_128[:, :], pattern=[[P, TT]], base=0, channel_multiplier=0,
                      allow_small_or_imprecise_dtypes=True).then_inc(const_bf, 1)
            pool.iota(ramp_tile[:, :], pattern=[[1, SLOT_TILES]], base=0, channel_multiplier=0,
                      allow_small_or_imprecise_dtypes=True).then_inc(const_bf, 1)
            pool.iota(token_id[:, :], pattern=[[P, TT]], base=0, channel_multiplier=1).then_inc(const_bf, 1)
            pool.memset(zero_row[:, :], 0.0).then_inc(fill_step, 1)
            pool.memset(pad_row[:, :], 0.0).then_inc(fill_step, 1)
            pool.wait_ge(fill_step, 2)
            pool.iota(pad_row[:, ID_COL:ID_COL + 1].bitcast(I32), pattern=[[0, 1]], base=T,
                      channel_multiplier=1).then_inc(fill_step, 1)
            pool.wait_ge(const_bf, 4)
            with pool.Fori(0, B) as b:
                for which in range(2):
                    pool.wait_ge(var_ready, 2 * b + which + 1)
                    pool.tensor_tensor(stats[:, :, 7:8], stats[:, :, 7:8], minus_half[:, :].rearrange("p (a o) -> p a o", o=1),
                                       ALU.pow).then_inc(inv_ready, 1)
                for half in range(HV):
                    pool.wait_ge(x_norm_ready, HV * b + half + 1)
                    pool.tensor_copy(rows1[:, bass.ds(HV * b + half, 1), 0:D],
                                     x_norm[:, half:half + 1, :])
                    pool.tensor_copy(rows2[:, bass.ds(HV * b + half, 1), 0:D],
                                     x_norm[:, half:half + 1, :]).then_inc(rows_ready, 1)
            pool.wait_ge(rt_done, 1)
            pool.wait_ge(rows_ready, TT + FREE)
            pool.wait_ge(st_fill, 16 * (SLOT_TILES + 1))
            for k, rows in enumerate((rows1, rows2)):
                for t in range(TT):
                    pool.indirect_dma_start(
                        out=slots[:, :], out_offset=bass.IndirectOffsetOnAxis(ap=pos[:, k, t:t + 1], axis=0),
                        in_=rows[:, t, :], in_offset=None).then_inc(st_rows, 16)
            pool.wait_ge(st_base, 16 * (TT + FREE))

            def add_tile(j, slot, y_slot):
                pool.wait_ge(r_ysb, j + 1)
                pool.sem_inc(pool_passed, 1)
                pool.indirect_dma_start(
                    out=out_rows[:, :],
                    out_offset=bass.IndirectOffsetOnAxis(ap=tile_in[:, slot, ID_COL:ID_COL + 1].bitcast(U32), axis=0),
                    in_=y_sb[:, y_slot, :], in_offset=None, compute_op=ALU.add).then_inc(r_add, 16)
                pool.wait_ge(r_add, 16 * (j + 1))

            with pool.Fori(0, SLOT_TILES // 6) as q:
                for s in range(6):
                    add_tile(6 * q + s, s % 3, s % 2)
            for j in range(SLOT_TILES - SLOT_TILES % 6, SLOT_TILES):
                add_tile(j, j % 3, j % 2)

        @block.tensor
        def _(pe):
            pe.wait_ge(const_ready, 1)
            pe.wait_ge(ld_w, 48)

            def attention_layer(b, layer):
                g = LAYERS * b + layer
                if layer == 0:
                    pe.wait_ge(ld_ctx, 16 * (b + 1))
                else:
                    pe.wait_ge(h0_copied, HV * (b + 1))
                for half in range(HV):
                    dst = ps_feat[:, half * D:(half + 1) * D]
                    if layer == 0:
                        mm = pe.matmul(dst, ctx_sb[0:F_IN, half * P:(half + 1) * P], w0_sb[0:F_IN, :],
                                       start=True, stop=True)
                    else:
                        for k in range(KC):
                            mm = pe.matmul(dst, h0_t[:, k, half * P:(half + 1) * P], w1_sb[:, k, :],
                                           start=(k == 0), stop=(k == KC - 1))
                mm.then_inc(feat_ready, 1)
                pe.wait_ge(parts_ready, g + 1)
                pe.sem_inc(pe_passed, 1)
                for side in range(2):
                    for half in range(HV):
                        i = side * HV + half
                        mm = pe.transpose(ps_tr[0:32, i * 64:(i + 1) * 64].bitcast(BF16),
                                          parts[:, half, side * 32:(side + 1) * 32], ident_bf[:, :])
                mm.then_inc(parts_turned, 1)
                pe.wait_ge(parts_copied, g + 1)

                def scores(u):
                    half, quad = u // 2, u % 2
                    w = UNITS * g + u
                    pe.wait_ge(z_copied, w + FREE)
                    for pair in range(QUAD // 2):
                        h = quad * QUAD + 2 * pair
                        dst = ps_z[:, pair * 512:(pair + 1) * 512]
                        pe.matmul(dst, parts_t[0:PARTS * HEADS, 0, half * P:(half + 1) * P],
                                  delta[0:PARTS * HEADS, h:h + 2, :], start=True, stop=False,
                                  skip_group_check=True)
                        for i in range(2):
                            mm = pe.matmul(dst[:, i * N:(i + 1) * N],
                                           delta[0:PARTS * HEADS, h + i, 0:P],
                                           parts_t[0:PARTS * HEADS, 1, :],
                                           start=False, stop=True, skip_group_check=True)
                    mm.then_inc(z_ready, 1)

                def turn(u):
                    w = UNITS * g + u
                    pe.wait_ge(probs_ready, w + 1)
                    pe.wait_ge(probs_copied, w + FREE)
                    for i in range(QUAD * HV):
                        mm = pe.transpose(ps_pt[:, i * P:(i + 1) * P], logits[:, u % 2, i * P:(i + 1) * P],
                                          ident[:, :])
                    mm.then_inc(probs_turned, 1)

                def weigh(u):
                    half, quad = u // 2, u % 2
                    w = UNITS * g + u
                    pe.wait_ge(probs_copied, w + 1 + FREE)
                    if u % 2 == 0:
                        pe.wait_ge(feat_copied, g + 1)
                    for i in range(QUAD):
                        h = quad * QUAD + i
                        for m in range(HV):
                            mm = pe.matmul(ps_o[:, half, h * FEATX:(h + 1) * FEATX],
                                           probs_t[:, u % 2, (i * HV + m) * P:(i * HV + m + 1) * P],
                                           featx[:, m, h * FEATX:(h + 1) * FEATX],
                                           start=(m == 0), stop=(m == HV - 1))
                    if quad == 1:
                        mm.then_inc(o_ready, 1)

                scores(0)
                for u in range(UNITS):
                    if u + 1 < UNITS:
                        scores(u + 1)
                    turn(u)
                    weigh(u)
                if layer == 0:
                    for half in range(HV):
                        pe.wait_ge(h0_ready, HV * b + half + 1)
                        for k in range(KC):
                            mm = pe.transpose(ps_tr[:, (half * KC + k) * P:(half * KC + k + 1) * P],
                                              h0[:, half, k * P:(k + 1) * P], ident[:, :])
                    mm.then_inc(h0_turned, 1)

            with pe.Fori(0, B) as b:
                attention_layer(b, 0)
                attention_layer(b, 1)
                for half in range(HV):
                    pe.wait_ge(x_norm_ready, HV * b + half + 1)
                    for k in range(KC):
                        mm = pe.transpose(ps_tr[:, (half * KC + k) * P:(half * KC + k + 1) * P],
                                          x_norm[:, half, k * P:(k + 1) * P], ident[:, :])
                mm.then_inc(x_norm_turned, 1)
                pe.wait_ge(x_norm_copied, b + 1)
                for half in range(HV):
                    for k in range(KC):
                        mm = pe.matmul(ps_feat[:, half * E:(half + 1) * E], x_norm_t[:, half, k, :],
                                       router_w[:, k, :], start=(k == 0), stop=(k == KC - 1))
                mm.then_inc(router_ready, 1)
                pe.wait_ge(ld_shared, 16)
                pe.wait_ge(router_exped, b + 1)
                for half in range(HV):
                    for e in range(NSH):
                        k = NSH * (HV * b + half) + e
                        base = (E + e) * W_EXP
                        for c, (c0, cw) in enumerate(GATE_CHUNKS):
                            slot = c % 2
                            if c == 2:
                                pe.wait_ge(hid_ready, 3 * k + 1)
                            for kc in range(KC):
                                a = base + kc * GU + 2 * c0
                                mm = pe.matmul(ps_gu[:, slot * 512:slot * 512 + 2 * cw], x_norm_t[:, half, kc, :],
                                               weights[:, a:a + 2 * cw], start=(kc == 0), stop=(kc == KC - 1))
                            mm.then_inc(gu_ready, 1)
                        pe.wait_ge(hid_ready, 3 * k + 3)
                        for c in range(IC):
                            mm = pe.transpose(ps_ht[:, c * P:(c + 1) * P], hid[:, e, c * P:(c + 1) * P], ident[:, :])
                        mm.then_inc(hid_turned, 1)
                        pe.wait_ge(hid_copied, k + 1)
                        for c in range(IC):
                            a = base + KC * GU + c * D
                            mm = pe.matmul(ps_y[:, 0:D], hid_t[:, e, c, :], weights[:, a:a + D],
                                           start=(e == 0 and c == 0), stop=(e == NSH - 1 and c == IC - 1))
                    mm.then_inc(y_ready, 1)
                    pe.wait_ge(y_saved, HV * b + half + 1)

            pe.wait_ge(rt_mm, 1)
            pe.matmul(ps_feat[:, 0:TT * E], below[:, :], both_bf[:, :], start=True, stop=True)
            pe.matmul(ps_tr[:, 0:TT * E], ones_bf[:, :], both_bf[:, :], start=True, stop=True).then_inc(router_ready, 1)
            pe.wait_ge(rt_done, 1)
            for e in range(E):
                pe.wait_ge(ld_expert[e], 16)

            def turn_in(j, s3, s2):
                for k in range(KC):
                    mm = pe.transpose(ps_tr[:, k * P:(k + 1) * P], tile_in[:, s3, k * P:(k + 1) * P], ident[:, :])
                mm.then_inc(r_xt, 1)

            def routed(j, s3, s2):
                pe.wait_ge(r_ld[s3], 16 * (j // 3 + 1) if isinstance(j, int) else j[0])
                jj = j if isinstance(j, int) else j[1]
                turn_in(jj, s3, s2)
                pe.wait_ge(r_xtc, jj + 1)
                ex = pe.value_load(expert_i[0:1, bass.ds(jj, 1)], min_val=0, max_val=E - 1)
                off = ex * W_EXP
                for c, (c0, cw) in enumerate(GATE_CHUNKS):
                    slot = c % 2
                    if c == 2:
                        pe.wait_ge(r_hid, 3 * jj + 1)
                    for kc in range(KC):
                        mm = pe.matmul(ps_gu[:, slot * 512:slot * 512 + 2 * cw], tile_t[:, s2, kc, :],
                                       weights[:, bass.ds(off + (kc * GU + 2 * c0), 2 * cw)],
                                       start=(kc == 0), stop=(kc == KC - 1))
                    mm.then_inc(r_gu, 1)
                pe.wait_ge(r_hid, 3 * jj + 3)
                for c in range(IC):
                    mm = pe.transpose(ps_ht[:, c * P:(c + 1) * P], hid[:, s2, c * P:(c + 1) * P], ident[:, :])
                mm.then_inc(r_ht, 1)
                pe.wait_ge(r_htc, jj + 1)
                for c in range(IC):
                    mm = pe.matmul(ps_y[:, 0:D], hid_t[:, s2, c, :],
                                   weights[:, bass.ds(off + (KC * GU + c * D), D)], start=(c == 0), stop=(c == IC - 1))
                mm.then_inc(r_y, 1)
                pe.wait_ge(r_ysb, jj + 1)

            with pe.Fori(0, SLOT_TILES // 6) as q:
                for s in range(6):
                    routed((16 * (2 * q + s // 3 + 1), 6 * q + s), s % 3, s % 2)
            for j in range(SLOT_TILES - SLOT_TILES % 6, SLOT_TILES):
                routed(j, j % 3, j % 2)

        @block.scalar
        def _(act):
            act.sem_inc(z_copied, FREE)
            act.sem_inc(st_base, 16 * FREE)
            act.wait_ge(ld_small, 16 * 8)
            act.activation(tanh_gates[:, :], gates[:, :], ACT.Tanh).then_inc(gates_ready, 1)
            act.dma_start(ctx_sb[0:F_IN, :], ctx_t[0]).then_inc(ld_ctx, 16)
            act.dma_start(x_in, x[0:N, :].rearrange("(h p) d -> p h d", p=P)).then_inc(ld_x, 16)

            def attention_layer(b, layer):
                g = LAYERS * b + layer
                act.wait_ge(feat_ready, g + 1)
                act.activation(
                    featx.rearrange("p a (h f) -> p a h f", h=HEADS)[:, :, :, 0:FO],
                    ps_feat[:, :].rearrange("p (a h f) -> p a h f", a=HV, h=HEADS), ACT.Copy).then_inc(feat_copied, 1)

                def copy_scores(u):
                    w = UNITS * g + u
                    act.wait_ge(z_ready, w + 1)
                    if u >= 2:
                        act.wait_ge(probs_turned, w - 1)
                    act.activation(logits[:, u % 2, :], ps_z[:, :], ACT.Copy).then_inc(z_copied, 1)

                def exponent(u):
                    w = UNITS * g + u
                    act.wait_ge(max_ready, w + 1)
                    for i in range(QUAD):
                        v = logits[:, u % 2, i * N:(i + 1) * N]
                        ins = act.activation(v, v, ACT.Exp, bias=neg_max[:, u % 2, i:i + 1], scale=-1.0)
                    ins.then_inc(probs_ready, 1)

                copy_scores(0)
                for u in range(UNITS):
                    if u + 1 < UNITS:
                        copy_scores(u + 1)
                    exponent(u)
                for half in range(HV):
                    act.wait_ge(min_ready, HV * g + half + 1)
                    act.activation(att_min[:, half, :], att_min[:, half, :], ACT.Exp).then_inc(exp_ready, 1)

            def after(b):
                act.wait_ge(x_norm_turned, b + 1)
                act.activation(x_norm_t[:, :, :, :].rearrange("p a k n -> p (a k n)"), ps_tr[:, :], ACT.Copy).then_inc(x_norm_copied, 1)
                act.wait_ge(router_ready, b + 1)
                act.activation(router_exp[:, bass.ds(HV * b, HV), :],
                               ps_feat[:, 0:HV * E].rearrange("p (a e) -> p a e", a=HV), ACT.Exp, scale=-1.0).then_inc(router_exped, 1)
                for half in range(HV):
                    for e in range(NSH):
                        k = NSH * (HV * b + half) + e
                        for c, (c0, cw) in enumerate(GATE_CHUNKS):
                            act.wait_ge(gu_ready, 3 * k + c + 1)
                            act.activation(gate_tanh[:, c % 2, 0:cw], ps_gu[:, (c % 2) * 512:(c % 2) * 512 + cw],
                                           ACT.Tanh, scale=0.5).then_inc(tanh_ready, 1)
                        act.wait_ge(hid_turned, k + 1)
                        act.activation(hid_t[:, e, :, :].rearrange("p a b -> p (a b)"), ps_ht[:, 0:I], ACT.Copy).then_inc(hid_copied, 1)

            with act.Fori(0, B - 1) as b:
                attention_layer(b, 0)
                act.dma_start(ctx_sb[0:F_IN, :], ctx_t[bass.ds(b + 1, 1)].rearrange("o f n -> (o f) n")).then_inc(ld_ctx, 16)
                attention_layer(b, 1)
                act.wait_ge(x_norm_ready, HV * (b + 1))
                act.dma_start(x_in, x[bass.ds((b + 1) * N, N), :].rearrange("(h p) d -> p h d", p=P)).then_inc(ld_x, 16)
                after(b)
                for half in range(HV):
                    act.wait_ge(y_saved, HV * b + half + 1)
                    act.dma_start(out_rows[bass.ds((HV * b + half) * P, P), :], y_sb[:, half, :]).then_inc(st_base, 16)
            b = B - 1
            attention_layer(b, 0)
            attention_layer(b, 1)
            after(b)
            for half in range(HV):
                act.wait_ge(y_saved, HV * b + half + 1)
                act.dma_start(out_rows[(HV * b + half) * P:(HV * b + half + 1) * P, :], y_sb[:, half, :]).then_inc(st_base, 16)

            def routed(j, s2):
                act.wait_ge(r_xt, j + 1)
                act.activation(tile_t[:, s2, :, :].rearrange("p a b -> p (a b)"), ps_tr[:, 0:D], ACT.Copy).then_inc(r_xtc, 1)
                for c, (c0, cw) in enumerate(GATE_CHUNKS):
                    act.wait_ge(r_gu, 3 * j + c + 1)
                    act.activation(gate_tanh[:, c % 2, 0:cw], ps_gu[:, (c % 2) * 512:(c % 2) * 512 + cw],
                                   ACT.Tanh, scale=0.5).then_inc(r_tanh, 1)
                act.wait_ge(r_ht, j + 1)
                act.activation(hid_t[:, s2, :, :].rearrange("p a b -> p (a b)"), ps_ht[:, 0:I], ACT.Copy).then_inc(r_htc, 1)

            with act.Fori(0, SLOT_TILES // 2) as q:
                for s in range(2):
                    routed(2 * q + s, s)
            for j in range(SLOT_TILES - SLOT_TILES % 2, SLOT_TILES):
                routed(j, j % 2)

        @block.vector
        def _(dve):
            count = [0]

            def link(ins, base):
                count[0] += 1
                ins.then_inc(dstep, 1)
                dve.wait_ge(dstep, base + count[0])

            dve.sem_inc(probs_copied, FREE)
            dve.wait_ge(const_ready, 1)
            dve.wait_ge(gates_ready, 1)

            def normalise(src, b, which, base):
                for half in range(HV):
                    dve.bn_stats(stats[:, half, 0:6], src[:, half, :]).then_inc(bn_ready, 1)
                dve.wait_ge(bn_ready, HV * (2 * b + which + 1))
                dve.sem_inc(dve_passed, 1)
                for half in range(HV):
                    ins = dve.bn_aggr(stats[:, half, 6:8], stats[:, half, 0:6])
                link(ins, base)
                dve.tensor_scalar(stats[:, :, 7:8], stats[:, :, 7:8], EPS, None, ALU.add).then_inc(var_ready, 1)
                dve.wait_ge(inv_ready, 2 * b + which + 1)

            def attention_layer(b, layer, base):
                g = LAYERS * b + layer
                dve.wait_ge(feat_copied, g + 1)
                for half in range(HV):
                    pv = prod[:, half, 0:2 * D].rearrange("p (s h f) -> p s h f", s=2, h=HEADS)
                    dve.tensor_tensor(pv,
                                      featx[:, half, :].rearrange("p (s h f) -> p s h f", s=1, h=HEADS)[:, :, :, 0:FO]
                                      .to_broadcast([P, 2, HEADS, FO]),
                                      a_sb[:, layer, :].rearrange("p (s h f) -> p s h f", s=2, h=HEADS), ALU.mult).then_inc(prod_ready, 1)
                dve.wait_ge(prod_ready, HV * (g + 1))
                link(dve.tensor_reduce(score.rearrange("p a s -> p (a s)"),
                                       prod[:, :, 0:2 * D].rearrange("p a (s f) -> p a s f", f=FO), AX.X, ALU.add), base)
                sv = score.rearrange("p a (s h) -> p a s h", s=2)
                rv = rest.rearrange("p a (s h) -> p a s h", s=2)

                def part(i):
                    return parts.rearrange("p a (s c) -> p a s c", s=2)[:, :, :, i * HEADS:(i + 1) * HEADS]

                link(dve.tensor_copy(part(0), sv), base)
                link(dve.tensor_tensor(rv, sv, part(0), ALU.subtract), base)
                link(dve.tensor_copy(part(1), rv), base)
                dve.tensor_tensor(part(2), rv, part(1), ALU.subtract).then_inc(parts_ready, 1)
                dve.wait_ge(parts_turned, g + 1)
                dve.tensor_copy(parts_t[0:32, :, :].rearrange("p s n -> p (s n)"),
                                ps_tr[0:32, 0:2 * HV * 64].bitcast(BF16)).then_inc(parts_copied, 1)

                def mask_max(u):
                    half = u // 2
                    w = UNITS * g + u
                    dve.wait_ge(z_copied, w + 1 + FREE)
                    if layer == 0 and u == 0:
                        dve.wait_ge(mask_ready, HV * (b + 1))
                    z = logits[:, u % 2, :]
                    dve.scalar_tensor_tensor(out=z, in0=z, scalar=LEAK, in1=z, op0=ALU.mult, op1=ALU.max
                                             ).then_inc(bent_ready, 1)
                    dve.wait_ge(bent_ready, w + 1)
                    dve.sem_inc(dve_passed, 1)
                    for i in range(QUAD):
                        v = logits[:, u % 2, i * N:(i + 1) * N]
                        ins = dve.tensor_tensor_reduce(v, v, mask[:, half, :], -1.0, BIG, ALU.add, ALU.min,
                                                       neg_max[:, u % 2, i:i + 1])
                    ins.then_inc(max_ready, 1)

                def copy_turned(u):
                    w = UNITS * g + u
                    dve.wait_ge(probs_turned, w + 1)
                    dve.tensor_copy(probs_t[:, u % 2, :], ps_pt[:, :]).then_inc(probs_copied, 1)

                def finish(half):
                    dve.wait_ge(o_ready, HV * g + half + 1)
                    ov = ps_o[:, half, 0:HEADS * FEATX].rearrange("p (h f) -> p h f", h=HEADS)
                    link(dve.reciprocal(o_inv[:, half, :].rearrange("p (h o) -> p h o", o=1), ov[:, :, FO:FEATX]), base)
                    av = att[:, half, :].rearrange("p (h f) -> p h f", h=HEADS)
                    link(dve.tensor_tensor(av, ov[:, :, 0:FO],
                                           o_inv[:, half, :].rearrange("p (h o) -> p h o", o=1).to_broadcast([P, HEADS, FO]),
                                           ALU.mult), base)
                    link(dve.tensor_tensor(att[:, half, :], att[:, half, :], bias_sb[:, layer, :], ALU.add), base)
                    dve.tensor_scalar(att_min[:, half, :], att[:, half, :], 0.0, None, ALU.min).then_inc(min_ready, 1)
                    link(dve.tensor_scalar(att[:, half, :], att[:, half, :], 0.0, None, ALU.max), base)
                    dve.wait_ge(exp_ready, HV * g + half + 1)
                    return dve.scalar_tensor_tensor(out=h0[:, half, :], in0=att_min[:, half, :], scalar=-1.0,
                                                    in1=att[:, half, :], op0=ALU.add, op1=ALU.add)

                mask_max(0)
                for u in range(UNITS):
                    if u + 1 < UNITS:
                        mask_max(u + 1)
                    copy_turned(u)
                for half in range(HV):
                    ins = finish(half)
                    if layer == 0:
                        ins.then_inc(h0_ready, 1)
                    else:
                        link(ins, base)
                if layer == 0:
                    dve.wait_ge(h0_turned, b + 1)
                    dve.tensor_copy(h0_t, ps_tr[:, :].rearrange("p (a k n) -> p k a n", a=HV, k=KC)
                                    ).then_inc(h0_copied, HV)

            def gelu_free_mul(ready_tanh, ready_silu, ready_hid, n, c, c0, cw, dst):
                s = c % 2
                dve.wait_ge(ready_tanh, n + 1)
                dve.scalar_tensor_tensor(out=gate_silu[:, s, 0:cw], in0=gate_tanh[:, s, 0:cw], scalar=1.0,
                                         in1=ps_gu[:, s * 512:s * 512 + cw], op0=ALU.add, op1=ALU.mult).then_inc(ready_silu, 1)
                dve.wait_ge(ready_silu, n + 1)
                dve.scalar_tensor_tensor(out=dst[:, c0:c0 + cw], in0=gate_silu[:, s, 0:cw], scalar=0.5,
                                         in1=ps_gu[:, s * 512 + cw:s * 512 + 2 * cw], op0=ALU.mult, op1=ALU.mult
                                         ).then_inc(ready_hid, 1)

            with dve.Fori(0, B) as b:
                count[0] = 0
                base = DSTEP_GRAPH * b
                dve.wait_ge(ld_x, 16 * (b + 1))
                normalise(x_in, b, 0, base)
                for half in range(HV):
                    link(dve.tensor_scalar(mask[:, half, :], x_in[:, half, :], stats[:, half, 6:7], stats[:, half, 7:8],
                                           ALU.subtract, ALU.mult), base)
                    dve.tensor_scalar(mask[:, half, :], mask[:, half, :], 1.0, MASK, ALU.subtract, ALU.mult
                                      ).then_inc(mask_ready, 1)
                attention_layer(b, 0, base)
                attention_layer(b, 1, base)
                for half in range(HV):
                    link(dve.scalar_tensor_tensor(out=x1[:, half, :], in0=h0[:, half, :], scalar=tanh_gates[:, 0:1],
                                                  in1=x_in[:, half, :], op0=ALU.mult, op1=ALU.add), base)
                normalise(x1, b, 1, base)
                dve.wait_ge(rows_ready, HV * b + FREE)
                for half in range(HV):
                    dve.tensor_scalar(x_norm[:, half, :], x1[:, half, :], stats[:, half, 6:7], stats[:, half, 7:8],
                                      ALU.subtract, ALU.mult
                                      ).then_inc(x_norm_ready, 1)
                for half in range(HV):
                    for e in range(NSH):
                        k = NSH * (HV * b + half) + e
                        for c, (c0, cw) in enumerate(GATE_CHUNKS):
                            gelu_free_mul(tanh_ready, silu_ready, hid_ready, 3 * k + c, c, c0, cw, hid[:, e, :])
                    dve.wait_ge(y_ready, HV * b + half + 1)
                    if half == 0:
                        dve.wait_ge(st_base, 16 * (HV * b + FREE))
                    dve.scalar_tensor_tensor(out=y_sb[:, half, :], in0=ps_y[:, 0:D], scalar=tanh_gates[:, 1:2],
                                             in1=x1[:, half, :], op0=ALU.mult, op1=ALU.add).then_inc(y_saved, 1)
                assert count[0] == DSTEP_GRAPH, count[0]

            n_rt = [0]

            def step(ins):
                n_rt[0] += 1
                ins.then_inc(rt_step, 1)
                dve.wait_ge(rt_step, n_rt[0])

            def per_tile(ap):
                return ap.rearrange("p (t o) -> p t o", o=1).to_broadcast([P, TT, E])

            def per_expert(ap, n=TT):
                return ap.rearrange("p (o e) -> p o e", o=1).to_broadcast([P, n, E])

            def te(ap):
                return ap.rearrange("p (t e) -> p t e", e=E)

            def tiles1(ap):
                return ap.rearrange("p (t o) -> p t o", o=1)

            dve.wait_ge(const_bf, 4)
            dve.wait_ge(router_exped, B)
            flat = score_r[:, :, :].rearrange("p t e -> p (t e)")
            step(dve.tensor_scalar(flat, router_exp[:, :, :].rearrange("p t e -> p (t e)"), 1.0, None, ALU.add))
            step(dve.reciprocal(flat, flat))
            for k in range(TOPK):
                step(dve.tensor_reduce(best[:, k, :], score_r[:, :, :], AX.X, ALU.max))
                step(dve.tensor_tensor(te(tmp_r[:, :]), score_r[:, :, :], per_tile(best[:, k, :]), ALU.is_equal))
                step(dve.tensor_tensor(te(tmp_r[:, :]), te(tmp_r[:, :]), per_expert(ramp_pri[:, :]), ALU.mult))
                step(dve.tensor_reduce(top_r[:, :], te(tmp_r[:, :]), AX.X, ALU.max))
                step(dve.tensor_tensor(te(sel[:, k, :]), te(tmp_r[:, :]), per_tile(top_r[:, :]), ALU.is_equal))
                if k == 0:
                    step(dve.scalar_tensor_tensor(out=flat, in0=sel[:, 0, :], scalar=-4.0, in1=flat,
                                                  op0=ALU.mult, op1=ALU.add))
            dve.tensor_tensor(both_bf[:, :], sel[:, 0, :], sel[:, 1, :], ALU.add).then_inc(rt_mm, 1)
            step(dve.tensor_tensor(top_r[:, :], best[:, 0, :], best[:, 1, :], ALU.add))
            step(dve.reciprocal(top_r[:, :], top_r[:, :]))
            dve.wait_ge(rows_ready, TT + FREE)
            for k, rows in enumerate((rows1, rows2)):
                step(dve.tensor_tensor(best[:, k, :], best[:, k, :], top_r[:, :], ALU.mult))
                dve.tensor_scalar(rows[:, :, W_COL:W_COL + 1], tiles1(best[:, k, :]), tanh_gates[:, 1:2], None, ALU.mult)
                dve.tensor_copy(rows[:, :, ID_COL:ID_COL + 1].bitcast(I32), tiles1(token_id[:, :]))
                dve.memset(rows[:, :, ID_COL + 1:ROW], 0.0)
            dve.wait_ge(router_ready, B + 1)
            step(dve.tensor_copy(counts[:, 0, :], ps_tr[:, 0:TT * E]))
            s = 0
            for shift in (1, 2, 4):
                a, b2 = counts[:, s, :], counts[:, 1 - s, :]
                dve.tensor_copy(b2[:, 0:shift * E], a[:, 0:shift * E])
                step(dve.tensor_tensor(b2[:, shift * E:], a[:, shift * E:], a[:, 0:(TT - shift) * E], ALU.add))
                s = 1 - s
            upto = counts[:, s, :]
            before = counts[:, 1 - s, :]
            total = upto[:, (TT - 1) * E:]
            step(dve.tensor_tensor(cmp_r[:, 0:E * TT].rearrange("p (e t) -> p e t", e=E),
                                   total.rearrange("p (e o) -> p e o", o=1).to_broadcast([P, E, TT]),
                                   ramp_128[:, :].rearrange("p (o t) -> p o t", o=1).to_broadcast([P, E, TT]), ALU.is_gt))
            step(dve.tensor_reduce(tiles_r[:, 0, :], cmp_r[:, 0:E * TT].rearrange("p (e t) -> p e t", e=E), AX.X, ALU.add))
            q = 0
            for shift in (1, 2, 4):
                a, b2 = tiles_r[:, q, :], tiles_r[:, 1 - q, :]
                dve.tensor_copy(b2[:, 0:shift], a[:, 0:shift])
                step(dve.tensor_tensor(b2[:, shift:], a[:, shift:], a[:, 0:E - shift], ALU.add))
                q = 1 - q
            ends = tiles_r[:, q, :]
            cv = cmp_r[:, :].rearrange("p (t e) -> p t e", e=E)
            step(dve.tensor_tensor(cv, per_expert(ends, SLOT_TILES),
                                   ramp_tile[:, :].rearrange("p (t o) -> p t o", o=1).to_broadcast([P, SLOT_TILES, E]), ALU.is_le))
            step(dve.tensor_reduce(expert_f[:, :], cv, AX.X, ALU.add))
            step(dve.tensor_scalar(expert_i[:, :], expert_f[:, :], float(E - 1), None, ALU.min))
            dve.memset(before[:, 0:E], 0.0)
            step(dve.tensor_copy(before[:, E:], upto[:, 0:(TT - 1) * E]))
            step(dve.tensor_tensor(before, before, ps_feat[:, 0:TT * E], ALU.add))
            start = tiles_r[:, 1 - q, :]
            dve.memset(start[:, 0:1], 0.0)
            step(dve.tensor_scalar(start[:, 1:E], ends[:, 0:E - 1], float(P), None, ALU.mult))
            step(dve.tensor_tensor(te(before), te(before), per_expert(start), ALU.add))
            for k in range(TOPK):
                step(dve.tensor_tensor(sel[:, k, :], sel[:, k, :], before, ALU.mult))
                step(dve.tensor_reduce(pos_f[:, k, :], te(sel[:, k, :]), AX.X, ALU.add))
            dve.tensor_copy(pos[:, :, :], pos_f[:, :, :]).then_inc(rt_done, 1)

            dve.wait_ge(st_base, 16 * (TT + FREE))
            def routed(j, s3, s2):
                for c, (c0, cw) in enumerate(GATE_CHUNKS):
                    gelu_free_mul(r_tanh, r_silu, r_hid, 3 * j + c, c, c0, cw, hid[:, s2, :])
                dve.wait_ge(r_y, j + 1)
                if isinstance(j, int) and j < 2:
                    pass
                else:
                    dve.wait_ge(r_add, 16 * (j - 1))
                dve.tensor_scalar(y_sb[:, s2, :], ps_y[:, 0:D], tile_in[:, s3, W_COL:W_COL + 1], None, ALU.mult
                                  ).then_inc(r_ysb, 1)

            for j in range(6):
                routed(j, j % 3, j % 2)
            with dve.Fori(1, SLOT_TILES // 6) as q6:
                for s6 in range(6):
                    routed(6 * q6 + s6, s6 % 3, s6 % 2)
            for j in range(SLOT_TILES - SLOT_TILES % 6, SLOT_TILES):
                routed(j, j % 3, j % 2)


def kernel(x, ctx_512, g_xattn, g_ffn, L0_xattn_W0, L0_xattn_a_self0, L0_xattn_a_neigh0, L0_xattn_b0,
           L0_xattn_W1, L0_xattn_a_self1, L0_xattn_a_neigh1, L0_xattn_b1, L0_ffn_w_router, L0_ffn_wg,
           L0_ffn_wu, L0_ffn_wd, L0_ffn_sg, L0_ffn_su, L0_ffn_sd):
    import numpy as np
    import concourse.bacc as bacc
    from concourse import mybir
    from concourse.bass_utils import run_bass_kernel_spmd

    def expert_rows(gate, up, down):
        n = gate.shape[0]
        g = np.asarray(gate).transpose(0, 2, 1).reshape(n, KC, P, I)
        u = np.asarray(up).transpose(0, 2, 1).reshape(n, KC, P, I)
        cols = []
        for c0, cw in GATE_CHUNKS:
            cols += [g[..., c0:c0 + cw], u[..., c0:c0 + cw]]
        gu = np.concatenate(cols, -1).transpose(0, 2, 1, 3).reshape(n, P, KC * GU)
        d = np.asarray(down).transpose(0, 2, 1).reshape(n, IC, P, D).transpose(0, 2, 1, 3).reshape(n, P, IC * D)
        return np.concatenate([gu, d], -1)

    arrays = {
        "x": np.asarray(x).reshape(T, D),
        "ctx_t": np.asarray(ctx_512).transpose(0, 2, 1),
        "w0": np.asarray(L0_xattn_W0).transpose(1, 0, 2).reshape(F_IN, HEADS * FO),
        "w1": np.asarray(L0_xattn_W1).transpose(1, 0, 2).reshape(D, HEADS * FO),
        "a_self0": np.asarray(L0_xattn_a_self0).reshape(-1),
        "a_neigh0": np.asarray(L0_xattn_a_neigh0).reshape(-1),
        "b0": np.asarray(L0_xattn_b0).reshape(-1),
        "a_self1": np.asarray(L0_xattn_a_self1).reshape(-1),
        "a_neigh1": np.asarray(L0_xattn_a_neigh1).reshape(-1),
        "b1": np.asarray(L0_xattn_b1).reshape(-1),
        "g_xattn": np.asarray(g_xattn).reshape(-1),
        "g_ffn": np.asarray(g_ffn).reshape(-1),
        "w_router": np.asarray(L0_ffn_w_router).transpose(1, 0),
        "w_experts": np.concatenate([expert_rows(L0_ffn_wg, L0_ffn_wu, L0_ffn_wd),
                                     expert_rows(L0_ffn_sg, L0_ffn_su, L0_ffn_sd)], 0),
    }
    arrays = {n: np.ascontiguousarray(a) for n, a in arrays.items()}
    nc = bacc.Bacc("TRN2", target_bir_lowering=False, num_devices=1)
    args = {n: nc.dram_tensor(n, a.shape, mybir.dt.from_np(a.dtype), kind="ExternalInput").ap()
            for n, a in arrays.items()}
    args["slots"] = nc.dram_tensor("slots", (SLOT_TILES * P, ROW), mybir.dt.float32, kind="Internal").ap()
    args["out"] = nc.dram_tensor("out", (T + P, D), mybir.dt.float32, kind="ExternalOutput").ap()
    build(nc, **args)
    r = run_bass_kernel_spmd(nc, [arrays], core_ids=[0])
    return r.results[0]["out"][0:T].reshape(B, N, D)
```

```python
from contextlib import ExitStack

import concourse.bass as bass
from concourse import mybir

F32 = mybir.dt.float32
BF16 = mybir.dt.bfloat16
U32 = mybir.dt.uint32
I32 = mybir.dt.int32
ALU = mybir.AluOpType
ACT = mybir.ActivationFunctionType
AX = mybir.AxisListType

P = 128
B, N, D = 4, 256, 256
F_IN = 64
HEADS, FO = 8, 32
E, NSH, I = 8, 2, 640
T = B * N
HV = N // P
TT = T // P
KC = D // P
IC = I // P
TOPK = 2
SLOT_TILES = TOPK * TT + E - 1
REGION = T + P
REGIONS = E + 1
ROW = D + 8
W_COL, ID_COL = D, D + 1
QUAD = 4
UNITS = HV * HEADS // QUAD
LAYERS = 2
LEAK = 0.2
MASK = 1e10
EPS = 1e-5
BIG = 3.0e38
GU = 2 * I
W_EXP = KC * GU + IC * D
GATE_CHUNKS = ((0, 256), (256, 256), (512, 128))
FEATX = FO + 1
PARTS = 3
SIDES = 2
PART_ROWS = 32 * PARTS
RAMPS = 10
PIECES = NSH * IC
SLOTS_IN = 6
PEELED = 4
ROUTED_LOOPS = (SLOT_TILES - 1 - PEELED) // SLOTS_IN
N_PARAMS = 2 * LAYERS * D + LAYERS * D + 2
FREE = 1
DSTEP_FIRST = 30
DSTEP_GRAPH = 54


def gate_col(i):
    c0, cw = GATE_CHUNKS[i * P // 256]
    return 2 * c0 + i * P - c0, 2 * c0 + cw + i * P - c0


def build(nc, x, ctx_t, w0, w1, params, w_router, w_experts, slots, out):
    with ExitStack() as stack:
        def sb(name, shape, dt=F32):
            return stack.enter_context(nc.sbuf_tensor(name, shape, dt))[(slice(None),) * len(shape)]

        def bank(name, shape, dt=F32):
            return stack.enter_context(nc.psum_tensor(name, shape, dt))[(slice(None),) * len(shape)]

        def sem(name):
            return stack.enter_context(nc.semaphore(name))

        weights = sb("weights", [P, (E + NSH) * W_EXP])
        rows = [sb(f"rows{k}", [P, HV, ROW]) for k in range(TOPK)]
        x_norm_t = sb("x_norm_t", [P, KC, N])
        x1 = sb("x1", [P, HV, D])
        ident = sb("ident", [P, P])
        router_w = sb("router_w", [P, KC, E])
        tanh_gates = sb("tanh_gates", [P, 2])
        hidden = sb("hidden", [P, NSH * IC * N])
        hid_shared = hidden.rearrange("p (e i n) -> p e i n", e=NSH, i=IC)
        hid = hidden[:, 0:2 * I].rearrange("p (s i) -> p s i", s=2)
        hid_t = hidden[:, 2 * I:4 * I].rearrange("p (s i n) -> p s i n", s=2, i=IC)
        gate_tanh = sb("gate_tanh", [P, 3, N])
        gate_silu = sb("gate_silu", [P, 3, N])
        y_sb = sb("y_sb", [P, HV, D])
        tile_in = sb("tile_in", [P, SLOTS_IN, ROW])
        tile_t = sb("tile_t", [P, 2, KC, P])
        w1_sb = sb("w1_sb", [P, KC, D])
        wa_sb = sb("wa_sb", [P, 1 + KC, PART_ROWS])

        LATE = 3
        scratch_at = [(E - LATE) * W_EXP]

        def carve(shape, dt=F32):
            n = 1
            for s in shape[1:]:
                n *= s
            n = n if dt == F32 else (n + 1) // 2
            a = scratch_at[0]
            scratch_at[0] = a + n
            assert scratch_at[0] <= E * W_EXP
            v = weights[:, a:a + n]
            if dt != F32:
                v = v.bitcast(dt)
            if len(shape) == 3:
                v = v.rearrange("p (a b) -> p a b", a=shape[1])
            return v

        x_in = carve([P, HV, D])
        mask = carve([P, HV, D])
        ctx_sb = carve([P, N])
        w0_sb = carve([P, D])
        params_sb = carve([P, N_PARAMS])
        pick_self = carve([P, HEADS, N], BF16)
        pick_neigh = carve([P, HEADS, P], BF16)
        featx = carve([P, HV, HEADS * FEATX])
        parts_t = carve([P, N], BF16)
        rest = carve([P, N])
        logits = carve([P, 2, QUAD * N])
        probs_t = carve([P, 2, QUAD * HV * P])
        neg_max = carve([P, 2, QUAD])
        stats = carve([P, HV, 8])
        o_inv = carve([P, HV, HEADS])
        att = carve([P, HV, D])
        att_min = carve([P, HV, D])
        h0_t = carve([P, KC, N])
        wa_prod = logits
        a_of = params_sb[:, 0:2 * LAYERS * D].rearrange("p (l s h f) -> p l s h f", l=LAYERS, s=SIDES, h=HEADS)
        bias_of = params_sb[:, 2 * LAYERS * D:3 * LAYERS * D].rearrange("p (l d) -> p l d", l=LAYERS)
        gates = params_sb[:, 3 * LAYERS * D:3 * LAYERS * D + 2]

        ps_z = bank("ps_z", [P, 2, 512])
        ps_pt = bank("ps_pt", [P, QUAD * HV * P])
        ps_a = bank("ps_a", [P, 512])
        ps_b = bank("ps_b", [P, 512])
        ps_gu = bank("ps_gu", [P, 512])
        ps_y = bank("ps_y", [P, 512])
        ps_o = (ps_a, ps_b)
        ps_chunk = (ps_z[:, 0, :], ps_z[:, 1, :], ps_gu)

        ld_x, ld_ctx, ld_w, ld_w1, ld_params = sem("ld_x"), sem("ld_ctx"), sem("ld_w"), sem("ld_w1"), sem("ld_params")
        ld_shared = sem("ld_shared")
        ld_expert = [sem(f"ld_expert{e}") for e in range(E)]
        const_step, ident_ready, ones_ready = sem("const_step"), sem("ident_ready"), sem("ones_ready")
        pick_ready, ramp_ready = sem("pick_ready"), sem("ramp_ready")
        gates_ready, wa_step, wa_ready = sem("gates_ready"), sem("wa_step"), sem("wa_ready")
        dstep, bn_ready, var_ready, inv_ready, mask_ready = sem("dstep"), sem("bn_ready"), sem("var_ready"), sem("inv_ready"), sem("mask_ready")
        dve_passed, pool_passed = sem("dve_passed"), sem("pool_passed")
        node_scores, feat_ready, feat_copied, parts_ready = sem("node_scores"), sem("feat_ready"), sem("feat_copied"), sem("parts_ready")
        z_ready, z_copied, bent_ready, max_ready = sem("z_ready"), sem("z_copied"), sem("bent_ready"), sem("max_ready")
        probs_ready, probs_turned, probs_copied = sem("probs_ready"), sem("probs_turned"), sem("probs_copied")
        o_ready, min_ready, exp_ready = sem("o_ready"), sem("min_ready"), sem("exp_ready")
        h0_ready, h0_turned, h0_copied = sem("h0_ready"), sem("h0_turned"), sem("h0_copied")
        x_norm_ready, x_norm_turned, x_norm_copied = sem("x_norm_ready"), sem("x_norm_turned"), sem("x_norm_copied")
        rows_copied, router_ready, router_exped = sem("rows_copied"), sem("router_ready"), sem("router_exped")
        both_ready, ranks_ready, sent_ready, st_rows = sem("both_ready"), sem("ranks_ready"), sem("sent_ready"), sem("st_rows")
        gu_ready, tanh_ready, silu_ready, hid_ready = sem("gu_ready"), sem("tanh_ready"), sem("silu_ready"), sem("hid_ready")
        y_ready, y_saved, st_base = sem("y_ready"), sem("y_saved"), sem("st_base")
        fill_step, st_fill, table_ready = sem("fill_step"), sem("st_fill"), sem("table_ready")
        r_gu, r_tanh, r_silu, r_hid = sem("r_gu"), sem("r_tanh"), sem("r_silu"), sem("r_hid")
        r_ht, r_htc, r_y, r_ysb = sem("r_ht"), sem("r_htc"), sem("r_y"), sem("r_ysb")
        r_ld = [sem(f"r_ld{i}") for i in range(SLOTS_IN)]
        r_xt, r_xtc, r_add = sem("r_xt"), sem("r_xtc"), sem("r_add")

        w_exp = weights.rearrange("p (e w) -> p e w", e=E + NSH)

        router_exp = sb("router_exp", [P, HV, E])
        score_r = sb("score_r", [P, HV, E])
        sel = sb("sel", [P, TOPK, HV * E])
        both_bf = sb("both_bf", [P, HV * E], BF16)
        tmp_r = sb("tmp_r", [P, HV * E])
        best = sb("best", [P, TOPK, HV])
        top_r = sb("top_r", [P, HV])
        before = sb("before", [P, HV * E])
        next_row = sb("next_row", [P, E])
        pos_f = sb("pos_f", [P, TOPK, HV])
        pos = sb("pos", [P, TOPK, HV], U32)
        token_id = sb("token_id", [P, HV])
        fill_r = sb("fill_r", [P, E])
        tiles_r = sb("tiles_r", [P, 3, E])
        cmp_r = sb("cmp_r", [P, SLOT_TILES * E])
        start_r = sb("start_r", [P, SLOT_TILES])
        expert_f = sb("expert_f", [P, SLOT_TILES])
        expert_i = sb("expert_i", [P, SLOT_TILES], I32)
        row_i = sb("row_i", [P, SLOT_TILES], I32)
        ramp_pri = sb("ramp_pri", [P, E])
        ramp_region = sb("ramp_region", [P, E])
        ramp_128 = sb("ramp_128", [P, TT])
        ramp_tile = sb("ramp_tile", [P, SLOT_TILES])
        pick8 = sb("pick8", [P, SIDES, HEADS])
        below = sb("below", [P, P], BF16)
        ones_bf = sb("ones_bf", [P, P], BF16)
        minus_half = sb("minus_half", [P, HV])
        pad_row = sb("pad_row", [P, ROW])
        zero_row = sb("zero_row", [P, D])

        block = stack.enter_context(nc.Block())

        @block.sync
        def _(sp):
            sp.dma_start(x_in, x[0:N, :].rearrange("(h p) d -> p h d", p=P)).then_inc(ld_x, 16)
            sp.dma_start(params_sb, params.rearrange("(o d) -> o d", o=1).to_broadcast([P, N_PARAMS])).then_inc(ld_params, 16)
            sp.dma_start(w1_sb, w1.rearrange("(k p) n -> p k n", p=P)).then_inc(ld_w1, 16)
            sp.dma_start(w_exp[:, E:E + NSH, :], w_experts[E:E + NSH].rearrange("e p w -> p e w")).then_inc(ld_shared, 16)
            def load_x(b):
                sp.wait_ge(x_norm_ready, HV * b)
                sp.dma_start(x_in, x[bass.ds(b * N, N), :].rearrange("(h p) d -> p h d", p=P)).then_inc(ld_x, 16)

            sp.wait_ge(fill_step, 3)
            fill = pad_row.rearrange("p (o r) -> p o r", o=1).to_broadcast([P, REGION // P, ROW])
            for e in range(REGIONS):
                sp.dma_start(slots[e * REGION:(e + 1) * REGION, :].rearrange("(k p) r -> p k r", p=P), fill).then_inc(st_fill, 16)
            sp.dma_start(out[T:T + P, :], zero_row).then_inc(st_fill, 16)
            load_x(1)
            for e in range(E - LATE):
                sp.dma_start(w_exp[:, e, :], w_experts[e]).then_inc(ld_expert[e], 16)
            for b in range(2, B):
                load_x(b)
            sp.wait_ge(x_norm_ready, HV * B)
            for e in range(E - LATE, E):
                sp.dma_start(w_exp[:, e, :], w_experts[e]).then_inc(ld_expert[e], 16)
            sp.wait_ge(st_rows, 16 * TOPK * TT)
            sp.wait_ge(table_ready, 1)

            def load_tile(j, slot):
                row = sp.value_load(row_i[0:1, bass.ds(j, 1)], min_val=0, max_val=REGION * REGIONS - P)
                sp.dma_start(tile_in[:, slot, :], slots[bass.ds(row, P), :]).then_inc(r_ld[slot], 16)

            for j in range(SLOTS_IN):
                load_tile(j, j)
            FULL = SLOT_TILES // SLOTS_IN - 1
            with sp.Fori(1, 1 + FULL) as q:
                for s in range(SLOTS_IN):
                    j = SLOTS_IN * q + s
                    sp.wait_ge(r_add, 16 * (j - SLOTS_IN + 1))
                    load_tile(j, s)
            for j in range(SLOTS_IN * (1 + FULL), SLOT_TILES):
                sp.wait_ge(r_add, 16 * (j - SLOTS_IN + 1))
                load_tile(j, j % SLOTS_IN)
            sp.wait_ge(r_add, 16 * SLOT_TILES)

        @block.gpsimd
        def _(pool):
            pool.memset(ident, 0.0).then_inc(const_step, 1)
            pool.memset(pick8, 0.0).then_inc(const_step, 1)
            pool.memset(wa_sb, 0.0).then_inc(const_step, 1)
            pool.memset(minus_half, -0.5).then_inc(const_step, 1)
            pool.memset(featx, 1.0).then_inc(ones_ready, 1)
            pool.wait_ge(const_step, 4)
            pool.affine_select(out=ident, in_=ident, compare_op=ALU.not_equal, fill=1.0, base=0,
                               pattern=[[-1, P]], channel_multiplier=1).then_inc(ident_ready, 1)
            for part in range(PARTS):
                if part > 0:
                    pool.wait_ge(pick_ready, SIDES * part)
                for side in range(SIDES):
                    v = pick8[:, side, :]
                    pool.affine_select(out=v, in_=v, compare_op=ALU.not_equal, fill=1.0,
                                       base=-(32 * part + side * HEADS), pattern=[[-1, HEADS]],
                                       channel_multiplier=1).then_inc(pick_ready, 1)
            pool.memset(ones_bf, 1.0).then_inc(ramp_ready, 1)
            pool.memset(below, 1.0).then_inc(const_step, 1)
            pool.wait_ge(const_step, 5)
            pool.affine_select(out=below, in_=below, compare_op=ALU.is_gt, fill=0.0, base=0,
                               pattern=[[1, P]], channel_multiplier=-1).then_inc(ramp_ready, 1)
            for ramp, step, first, mult in ((ramp_pri, -1, E, 0), (ramp_128, P, 0, 0), (ramp_tile, 1, 0, 0),
                                            (ramp_region, REGION, 0, 0), (next_row, REGION, 0, 0), (token_id, P, 0, 1)):
                pool.iota(ramp, pattern=[[step, ramp.shape[1]]], base=first, channel_multiplier=mult,
                          allow_small_or_imprecise_dtypes=True).then_inc(ramp_ready, 1)
            pool.memset(zero_row, 0.0).then_inc(fill_step, 1)
            pool.memset(pad_row, 0.0).then_inc(fill_step, 1)
            pool.wait_ge(fill_step, 2)
            pool.iota(pad_row[:, ID_COL:ID_COL + 1].bitcast(I32), pattern=[[0, 1]], base=T,
                      channel_multiplier=1).then_inc(fill_step, 1)
            for k in range(TOPK):
                pool.memset(rows[k][:, :, ID_COL + 1:ROW], 0.0).then_inc(ramp_ready, 1)

            def power(b, which):
                pool.wait_ge(var_ready, 2 * b + which + 1)
                pool.tensor_tensor(stats[:, :, 7:8], stats[:, :, 7:8], minus_half.rearrange("p (a o) -> p a o", o=1),
                                   ALU.pow).then_inc(inv_ready, 1)

            def copy_rows(b):
                pool.wait_ge(x_norm_ready, HV * b + HV)
                pool.sem_inc(pool_passed, 1)
                pool.tensor_copy(rows[1][:, :, 0:D], rows[0][:, :, 0:D]).then_inc(rows_copied, 1)

            def send_rows(b):
                pool.wait_ge(sent_ready, b + 1)
                pool.sem_inc(pool_passed, 1)
                for k in range(TOPK):
                    for half in range(HV):
                        pool.indirect_dma_start(
                            out=slots, out_offset=bass.IndirectOffsetOnAxis(ap=pos[:, k, half:half + 1], axis=0),
                            in_=rows[k][:, half, :], in_offset=None).then_inc(st_rows, 16)

            power(0, 0)
            power(0, 1)
            copy_rows(0)
            pool.wait_ge(st_fill, 16 * (REGIONS + 1))
            with pool.Fori(1, B) as b:
                power(b, 0)
                send_rows(b - 1)
                power(b, 1)
                copy_rows(b)
            send_rows(B - 1)
            pool.wait_ge(st_base, 16 * (B + FREE))

            def add_tile(j, slot, y_slot):
                pool.wait_ge(r_ysb, j + 1)
                pool.sem_inc(pool_passed, 1)
                pool.indirect_dma_start(
                    out=out, out_offset=bass.IndirectOffsetOnAxis(ap=tile_in[:, slot, ID_COL:ID_COL + 1].bitcast(U32), axis=0),
                    in_=y_sb[:, y_slot, :], in_offset=None, compute_op=ALU.add).then_inc(r_add, 16)
                pool.wait_ge(r_add, 16 * (j + 1))

            with pool.Fori(0, SLOT_TILES // SLOTS_IN) as q:
                for s in range(SLOTS_IN):
                    add_tile(SLOTS_IN * q + s, s, s % 2)
            for j in range(SLOT_TILES - SLOT_TILES % SLOTS_IN, SLOT_TILES):
                add_tile(j, j % SLOTS_IN, j % 2)

        @block.tensor
        def _(pe):
            def no_piece():
                pass

            def attention_layer(b, layer, piece):
                g = LAYERS * b + layer
                if layer == 0:
                    pe.wait_ge(ld_ctx, 16 * (b + 1))
                    if not isinstance(b, int):
                        pe.wait_ge(router_exped, b)
                    src = [(ctx_sb[0:F_IN, :], w0_sb[0:F_IN, :], wa_sb[0:F_IN, 0, :])]
                else:
                    pe.wait_ge(h0_copied, b + 1)
                    src = [(h0_t[:, k, :], w1_sb[:, k, :], wa_sb[:, 1 + k, :]) for k in range(KC)]
                for k, (v, w, wa) in enumerate(src):
                    mm = pe.matmul(ps_b[0:PART_ROWS, 0:N], wa, v, start=(k == 0), stop=(k == len(src) - 1))
                mm.then_inc(node_scores, 1)
                for half in range(HV):
                    for k, (v, w, wa) in enumerate(src):
                        mm = pe.matmul(ps_a[:, half * D:(half + 1) * D], v[:, half * P:(half + 1) * P], w,
                                       start=(k == 0), stop=(k == len(src) - 1))
                mm.then_inc(feat_ready, 1)
                piece()
                pe.wait_ge(parts_ready, g + 1)

                def scores(u):
                    half, quad = u // 2, u % 2
                    pe.wait_ge(z_copied, UNITS * g + u + FREE)
                    for pair in range(QUAD // 2):
                        h = quad * QUAD + 2 * pair
                        pe.matmul(ps_z[:, pair, :], parts_t[0:PART_ROWS, half * P:(half + 1) * P],
                                  pick_self[0:PART_ROWS, h:h + 2, :], start=True, stop=False, skip_group_check=True)
                        for i in range(2):
                            mm = pe.matmul(ps_z[:, pair, i * N:(i + 1) * N], pick_neigh[0:PART_ROWS, h + i, :],
                                           parts_t[0:PART_ROWS, :], start=False, stop=True, skip_group_check=True)
                    mm.then_inc(z_ready, 1)

                def turn(u):
                    w = UNITS * g + u
                    pe.wait_ge(probs_ready, w + 1)
                    pe.wait_ge(probs_copied, w + FREE)
                    for i in range(QUAD * HV):
                        mm = pe.transpose(ps_pt[:, i * P:(i + 1) * P], logits[:, u % 2, i * P:(i + 1) * P], ident)
                    mm.then_inc(probs_turned, 1)

                def weigh(u):
                    half, quad = u // 2, u % 2
                    pe.wait_ge(probs_copied, UNITS * g + u + 1 + FREE)
                    for i in range(QUAD):
                        h = quad * QUAD + i
                        for m in range(HV):
                            mm = pe.matmul(ps_o[half][:, h * FEATX:(h + 1) * FEATX],
                                           probs_t[:, u % 2, (i * HV + m) * P:(i * HV + m + 1) * P],
                                           featx[:, m, h * FEATX:(h + 1) * FEATX],
                                           start=(m == 0), stop=(m == HV - 1))
                    if quad == 1:
                        mm.then_inc(o_ready, 1)

                scores(0)
                piece()
                scores(1)
                for u in range(UNITS):
                    turn(u)
                    if u + 2 < UNITS:
                        scores(u + 2)
                    piece()
                    if u == 0:
                        pe.wait_ge(feat_copied, g + 1)
                    weigh(u)
                piece()
                if layer == 0:
                    pe.wait_ge(h0_ready, HV * b + HV)
                    for half in range(HV):
                        for k in range(KC):
                            mm = pe.transpose(ps_b[:, (half * KC + k) * P:(half * KC + k + 1) * P],
                                              att[:, half, k * P:(k + 1) * P], ident)
                    mm.then_inc(h0_turned, 1)

            def after_attention(b):
                pe.wait_ge(x_norm_ready, HV * b + HV)
                for half in range(HV):
                    for k in range(KC):
                        mm = pe.transpose(ps_b[:, (k * HV + half) * P:(k * HV + half + 1) * P],
                                          rows[0][:, half, k * P:(k + 1) * P], ident)
                mm.then_inc(x_norm_turned, 1)
                pe.wait_ge(x_norm_copied, b + 1)
                for half in range(HV):
                    for k in range(KC):
                        mm = pe.matmul(ps_a[:, half * E:(half + 1) * E], x_norm_t[:, k, half * P:(half + 1) * P],
                                       router_w[:, k, :], start=(k == 0), stop=(k == KC - 1))
                mm.then_inc(router_ready, 1)

            def ranks(b):
                pe.wait_ge(both_ready, b + 1)
                first, second = both_bf[:, 0:E], both_bf[:, E:2 * E]
                pe.matmul(ps_y[:, 0:E], below, first, start=True, stop=True)
                pe.matmul(ps_y[:, E:2 * E], below, second, start=True, stop=False)
                pe.matmul(ps_y[:, E:2 * E], ones_bf, first, start=False, stop=True)
                pe.matmul(ps_y[:, 2 * E:3 * E], ones_bf, first, start=True, stop=False)
                pe.matmul(ps_y[:, 2 * E:3 * E], ones_bf, second, start=False, stop=True).then_inc(ranks_ready, 1)

            def gate_up(c, i, dst, behind):
                n = PIECES * c + i
                if i >= behind:
                    pe.wait_ge(hid_ready, n + 1 - behind)
                base = (E + i // IC) * W_EXP
                for part, col in enumerate(gate_col(i % IC)):
                    for k in range(KC):
                        a = base + k * GU + col
                        mm = pe.matmul(dst[:, part * N:(part + 1) * N], weights[:, a:a + P],
                                       x_norm_t[:, k, :], start=(k == 0), stop=(k == KC - 1))
                mm.then_inc(gu_ready, 1)

            def down(c, half, e):
                if half == 0:
                    pe.wait_ge(hid_ready, PIECES * c + IC * (e + 1))
                    if e == 0:
                        pe.wait_ge(sent_ready, c + 1)
                for i in range(IC):
                    a = (E + e) * W_EXP + KC * GU + i * D
                    mm = pe.matmul(ps_y[:, half * D:(half + 1) * D], hid_shared[:, e, i, half * P:(half + 1) * P],
                                   weights[:, a:a + D], start=(e == 0 and i == 0), stop=(e == NSH - 1 and i == IC - 1))
                if half == HV - 1 and e == NSH - 1:
                    mm.then_inc(y_ready, 1)

            pe.wait_ge(ident_ready, 1)
            pe.wait_ge(ld_w, 32)
            pe.wait_ge(wa_ready, 1)
            attention_layer(0, 0, no_piece)
            pe.wait_ge(ld_w1, 16)
            attention_layer(0, 1, no_piece)
            after_attention(0)
            pe.wait_ge(ld_shared, 16)
            with pe.Fori(1, B) as b:
                todo = list(range(PIECES)) + [(half, e) for half in range(HV) for e in range(NSH)]

                def piece():
                    t = todo.pop(0)
                    if isinstance(t, int):
                        gate_up(b - 1, t, ps_gu, 1)
                    else:
                        down(b - 1, *t)

                attention_layer(b, 0, piece)
                ranks(b - 1)
                attention_layer(b, 1, piece)
                assert not todo
                after_attention(b)
            for i in range(PIECES):
                gate_up(B - 1, i, ps_chunk[i % 3], 3)
                if i == 2:
                    ranks(B - 1)
            for half in range(HV):
                for e in range(NSH):
                    down(B - 1, half, e)

            for e in range(E):
                pe.wait_ge(ld_expert[e], 16)

            def turn_in(q, r):
                j = SLOTS_IN * q + r
                pe.wait_ge(r_ld[r % SLOTS_IN], 16 * (q + r // SLOTS_IN + 1))
                if not isinstance(j, int) or j >= 1:
                    pe.wait_ge(r_xtc, j)
                for k in range(KC):
                    mm = pe.transpose(ps_b[:, k * P:(k + 1) * P], tile_in[:, r % SLOTS_IN, k * P:(k + 1) * P], ident)
                mm.then_inc(r_xt, 1)

            def gate_chunk(q, r, c, off):
                j = SLOTS_IN * q + r
                c0, cw = GATE_CHUNKS[c]
                if c == 0:
                    pe.wait_ge(r_xtc, j + 1)
                if not isinstance(j, int) or j >= 1:
                    pe.wait_ge(r_hid, 3 * j + c - 2)
                for k in range(KC):
                    mm = pe.matmul(ps_chunk[c][:, 0:2 * cw], tile_t[:, r % 2, k, :],
                                   weights[:, bass.ds(off + (k * GU + 2 * c0), 2 * cw)],
                                   start=(k == 0), stop=(k == KC - 1))
                mm.then_inc(r_gu, 1)

            def expert_at(q, r):
                e = pe.value_load(expert_i[0:1, bass.ds(SLOTS_IN * q + r, 1)], min_val=0, max_val=E - 1)
                return e * W_EXP

            def turn_hidden(q, r):
                j = SLOTS_IN * q + r
                pe.wait_ge(r_hid, 3 * j + 3)
                if not isinstance(j, int) or j >= 1:
                    pe.wait_ge(r_htc, j)
                for i in range(IC):
                    mm = pe.transpose(ps_pt[:, i * P:(i + 1) * P], hid[:, r % 2, i * P:(i + 1) * P], ident)
                mm.then_inc(r_ht, 1)

            def down_tile(q, r):
                j = SLOTS_IN * q + r
                off = expert_at(q, r)
                pe.wait_ge(r_htc, j + 1)
                if not isinstance(j, int) or j >= 1:
                    pe.wait_ge(r_ysb, j)
                for i in range(IC):
                    mm = pe.matmul(ps_y[:, 0:D], hid_t[:, r % 2, i, :],
                                   weights[:, bass.ds(off + (KC * GU + i * D), D)], start=(i == 0), stop=(i == IC - 1))
                mm.then_inc(r_y, 1)

            def step(q, r):
                s = SLOTS_IN * q + r
                inner = not isinstance(s, int)
                off = expert_at(q, r) if inner or s < SLOT_TILES else None
                if off is not None:
                    gate_chunk(q, r, 0, off)
                if inner or s >= 2:
                    down_tile(q, r - 2)
                if off is not None:
                    gate_chunk(q, r, 1, off)
                    gate_chunk(q, r, 2, off)
                if inner or s + 1 < SLOT_TILES:
                    turn_in(q, r + 1)
                if inner or 1 <= s <= SLOT_TILES:
                    turn_hidden(q, r - 1)

            pe.wait_ge(table_ready, 1)
            pe.wait_ge(y_saved, B)
            turn_in(0, 0)
            for s in range(PEELED):
                step(0, s)
            with pe.Fori(0, ROUTED_LOOPS) as q:
                for r in range(PEELED, PEELED + SLOTS_IN):
                    step(q, r)
            for s in range(PEELED + SLOTS_IN * ROUTED_LOOPS, SLOT_TILES + 2):
                step(0, s)

        @block.scalar
        def _(act):
            act.sem_inc(z_copied, FREE)
            act.sem_inc(probs_copied, FREE)
            act.sem_inc(st_base, 16 * FREE)
            act.dma_start(ctx_sb[0:F_IN, :], ctx_t[0]).then_inc(ld_ctx, 16)
            act.dma_start(w0_sb[0:F_IN, :], w0).then_inc(ld_w, 16)
            act.dma_start(router_w, w_router.rearrange("(k p) e -> p k e", p=P)).then_inc(ld_w, 16)
            act.wait_ge(ld_params, 16)
            act.activation(tanh_gates, gates, ACT.Tanh).then_inc(gates_ready, 1)
            act.wait_ge(ones_ready, 1)

            def no_piece():
                pass

            def attention_layer(b, layer, piece):
                g = LAYERS * b + layer
                act.wait_ge(feat_ready, g + 1)
                act.activation(
                    featx.rearrange("p a (h f) -> p a h f", h=HEADS)[:, :, :, 0:FO],
                    ps_a.rearrange("p (a h f) -> p a h f", a=HV, h=HEADS), ACT.Copy).then_inc(feat_copied, 1)
                piece()

                def copy_scores(u):
                    w = UNITS * g + u
                    act.wait_ge(z_ready, w + 1)
                    if u >= 2:
                        act.wait_ge(probs_turned, w - 1)
                    act.activation(logits[:, u % 2, :], ps_z.rearrange("p a n -> p (a n)"), ACT.Copy).then_inc(z_copied, 1)

                def exponent(u):
                    act.wait_ge(max_ready, UNITS * g + u + 1)
                    for i in range(QUAD):
                        v = logits[:, u % 2, i * N:(i + 1) * N]
                        ins = act.activation(v, v, ACT.Exp, bias=neg_max[:, u % 2, i:i + 1], scale=-1.0)
                    ins.then_inc(probs_ready, 1)

                def copy_turned(u):
                    act.wait_ge(probs_turned, UNITS * g + u + 1)
                    act.activation(probs_t[:, u % 2, :], ps_pt, ACT.Copy).then_inc(probs_copied, 1)

                copy_scores(0)
                piece()
                copy_scores(1)
                for u in range(UNITS):
                    exponent(u)
                    if u > 0:
                        piece()
                    copy_turned(u)
                    if u + 2 < UNITS:
                        copy_scores(u + 2)
                piece()
                piece()
                for half in range(HV):
                    act.wait_ge(min_ready, HV * g + half + 1)
                    act.activation(att_min[:, half, :], att_min[:, half, :], ACT.Exp).then_inc(exp_ready, 1)
                if layer == 0:
                    act.wait_ge(h0_turned, b + 1)
                    act.activation(h0_t, ps_b.rearrange("p (a k n) -> p k a n", a=HV, k=KC), ACT.Copy).then_inc(h0_copied, 1)

            def after_attention(b):
                act.wait_ge(x_norm_turned, b + 1)
                v = ps_b.rearrange("p (k n) -> p k n", k=KC)
                act.activation(x_norm_t, v, ACT.Copy).then_inc(x_norm_copied, 1)
                act.wait_ge(router_ready, b + 1)
                act.activation(router_exp, ps_a[:, 0:HV * E].rearrange("p (a e) -> p a e", a=HV), ACT.Exp, scale=-1.0).then_inc(router_exped, 1)

            def tanh_piece(c, i, src, s):
                act.wait_ge(gu_ready, PIECES * c + i + 1)
                act.activation(gate_tanh[:, s, :], src[:, 0:N], ACT.Tanh, scale=0.5).then_inc(tanh_ready, 1)

            attention_layer(0, 0, no_piece)
            act.dma_start(ctx_sb[0:F_IN, :], ctx_t[1]).then_inc(ld_ctx, 16)
            attention_layer(0, 1, no_piece)
            after_attention(0)

            def loop_body(b, more):
                todo = list(range(PIECES))

                def piece():
                    if todo:
                        tanh_piece(b - 1, todo.pop(0), ps_gu, 0)

                attention_layer(b, 0, piece)
                if more:
                    act.dma_start(ctx_sb[0:F_IN, :], ctx_t[bass.ds(b + 1, 1)].rearrange("o f n -> (o f) n")).then_inc(ld_ctx, 16)
                attention_layer(b, 1, piece)
                assert not todo
                after_attention(b)
                act.wait_ge(y_saved, b)
                act.dma_start(out[bass.ds((b - 1) * N, N), :].rearrange("(h p) d -> p h d", p=P), y_sb).then_inc(st_base, 16)

            with act.Fori(1, B - 1) as b:
                loop_body(b, True)
            loop_body(B - 1, False)
            for i in range(PIECES):
                tanh_piece(B - 1, i, ps_chunk[i % 3], i % 3)
            act.wait_ge(y_saved, B)
            act.dma_start(out[(B - 1) * N:B * N, :].rearrange("(h p) d -> p h d", p=P), y_sb).then_inc(st_base, 16)

            def copy_in(q, r):
                act.wait_ge(r_xt, SLOTS_IN * q + r + 1)
                act.activation(tile_t[:, r % 2, :, :].rearrange("p a b -> p (a b)"), ps_b[:, 0:D], ACT.Copy).then_inc(r_xtc, 1)

            def step(q, r):
                s = SLOTS_IN * q + r
                inner = not isinstance(s, int)
                if inner or s < SLOT_TILES:
                    for c, (c0, cw) in enumerate(GATE_CHUNKS):
                        act.wait_ge(r_gu, 3 * s + c + 1)
                        act.activation(gate_tanh[:, c, 0:cw], ps_chunk[c][:, 0:cw], ACT.Tanh, scale=0.5).then_inc(r_tanh, 1)
                if inner or s + 1 < SLOT_TILES:
                    copy_in(q, r + 1)
                if inner or s >= 1:
                    act.wait_ge(r_ht, s)
                    act.activation(hid_t[:, (r - 1) % 2, :, :].rearrange("p a b -> p (a b)"), ps_pt[:, 0:I], ACT.Copy
                                   ).then_inc(r_htc, 1)

            copy_in(0, 0)
            for s in range(PEELED):
                step(0, s)
            with act.Fori(0, ROUTED_LOOPS) as q:
                for r in range(PEELED, PEELED + SLOTS_IN):
                    step(q, r)
            for s in range(PEELED + SLOTS_IN * ROUTED_LOOPS, SLOT_TILES + 1):
                step(0, s)

        @block.vector
        def _(dve):
            count = [0]
            base = [0]

            def link(ins):
                count[0] += 1
                ins.then_inc(dstep, 1)
                dve.wait_ge(dstep, base[0] + count[0])

            def start_count(done):
                count[0] = 0
                base[0] = done

            dve.wait_ge(ld_params, 16)
            dve.wait_ge(ld_w, 32)
            dve.wait_ge(ld_w1, 16)
            dve.wait_ge(const_step, 4)
            n_wa = 0
            for layer, k, w, np_ in ((0, 0, w0_sb, F_IN), (1, 1, w1_sb[:, 0, :], P), (1, 2, w1_sb[:, 1, :], P)):
                prod = wa_prod.rearrange("p a b -> p (a b)")[0:np_, k * 512:(k + 1) * 512]
                dve.tensor_tensor(prod.rearrange("p (s h f) -> p s h f", s=SIDES, h=HEADS),
                                  w[0:np_, :].rearrange("p (s h f) -> p s h f", s=1, h=HEADS).to_broadcast([np_, SIDES, HEADS, FO]),
                                  a_of[0:np_, layer], ALU.mult).then_inc(wa_step, 1)
                n_wa += 1
                dve.wait_ge(wa_step, n_wa)
                ins = dve.tensor_reduce(wa_sb[0:np_, k, 0:SIDES * HEADS], prod.rearrange("p (s f) -> p s f", f=FO), AX.X, ALU.add)
                ins.then_inc(wa_step, 1)
                n_wa += 1
                dve.wait_ge(wa_step, n_wa)
                for part in range(1, PARTS):
                    ins = dve.tensor_copy(wa_sb[0:np_, k, 32 * part:32 * part + SIDES * HEADS], wa_sb[0:np_, k, 0:SIDES * HEADS])
            ins.then_inc(wa_ready, 1)
            dve.wait_ge(pick_ready, SIDES * PARTS)
            dve.tensor_copy(pick_self, pick8[:, 0, :].rearrange("p (h o) -> p h o", o=1).to_broadcast([P, HEADS, N]))
            dve.tensor_copy(pick_neigh, pick8[:, 1, :].rearrange("p (h o) -> p h o", o=1).to_broadcast([P, HEADS, P]))

            def normalise(src, b, which):
                for half in range(HV):
                    dve.bn_stats(stats[:, half, 0:6], src[:, half, :]).then_inc(bn_ready, 1)
                dve.wait_ge(bn_ready, HV * (2 * b + which + 1))
                dve.sem_inc(dve_passed, 1)
                for half in range(HV):
                    ins = dve.bn_aggr(stats[:, half, 6:8], stats[:, half, 0:6])
                link(ins)
                dve.tensor_scalar(stats[:, :, 7:8], stats[:, :, 7:8], EPS, None, ALU.add).then_inc(var_ready, 1)
                dve.wait_ge(inv_ready, 2 * b + which + 1)

            def make_mask(b):
                dve.wait_ge(ld_x, 16 * (b + 1))
                normalise(x_in, b, 0)
                for half in range(HV):
                    link(dve.tensor_scalar(mask[:, half, :], x_in[:, half, :], stats[:, half, 6:7], stats[:, half, 7:8],
                                           ALU.subtract, ALU.mult))
                    dve.tensor_scalar(mask[:, half, :], mask[:, half, :], 1.0, MASK, ALU.subtract, ALU.mult
                                      ).then_inc(mask_ready, 1)

            def attention_layer(b, layer, piece, between):
                g = LAYERS * b + layer
                dve.wait_ge(node_scores, g + 1)
                z = ps_b[0:PART_ROWS, 0:N]
                link(dve.tensor_copy(parts_t[0:PART_ROWS, :], z))
                link(dve.tensor_tensor(rest[0:PART_ROWS, :], z, parts_t[0:PART_ROWS, :], ALU.subtract))
                link(dve.tensor_copy(parts_t[0:64, :], rest[0:64, :]))
                dve.tensor_tensor(parts_t[0:32, :], rest[0:32, :], parts_t[0:32, :], ALU.subtract).then_inc(parts_ready, 1)
                between()
                piece()

                def mask_max(u):
                    half = u // 2
                    w = UNITS * g + u
                    dve.wait_ge(z_copied, w + 1 + FREE)
                    if layer == 0 and u == 0:
                        dve.wait_ge(mask_ready, HV * (b + 1))
                    z = logits[:, u % 2, :]
                    dve.scalar_tensor_tensor(out=z, in0=z, scalar=LEAK, in1=z, op0=ALU.mult, op1=ALU.max
                                             ).then_inc(bent_ready, 1)
                    dve.wait_ge(bent_ready, w + 1)
                    dve.sem_inc(dve_passed, 1)
                    for i in range(QUAD):
                        v = logits[:, u % 2, i * N:(i + 1) * N]
                        ins = dve.tensor_tensor_reduce(v, v, mask[:, half, :], -1.0, BIG, ALU.add, ALU.min,
                                                       neg_max[:, u % 2, i:i + 1])
                    ins.then_inc(max_ready, 1)

                def finish(half):
                    dve.wait_ge(o_ready, HV * g + half + 1)
                    ov = ps_o[half][:, 0:HEADS * FEATX].rearrange("p (h f) -> p h f", h=HEADS)
                    inv = o_inv[:, half, :].rearrange("p (h o) -> p h o", o=1)
                    link(dve.reciprocal(inv, ov[:, :, FO:FEATX]))
                    av = att[:, half, :].rearrange("p (h f) -> p h f", h=HEADS)
                    link(dve.tensor_tensor(av, ov[:, :, 0:FO], inv.to_broadcast([P, HEADS, FO]), ALU.mult))
                    link(dve.tensor_tensor(att[:, half, :], att[:, half, :], bias_of[:, layer, :], ALU.add))
                    dve.tensor_scalar(att_min[:, half, :], att[:, half, :], 0.0, None, ALU.min).then_inc(min_ready, 1)
                    link(dve.tensor_scalar(att[:, half, :], att[:, half, :], 0.0, None, ALU.max))

                def elu(half):
                    dve.wait_ge(exp_ready, HV * g + half + 1)
                    ins = dve.scalar_tensor_tensor(out=att[:, half, :], in0=att_min[:, half, :], scalar=-1.0,
                                                   in1=att[:, half, :], op0=ALU.add, op1=ALU.add)
                    if layer == 0:
                        ins.then_inc(h0_ready, 1)
                    else:
                        link(ins)

                mask_max(0)
                piece()
                mask_max(1)
                for u in range(2, UNITS):
                    piece()
                    mask_max(u)
                piece()
                finish(0)
                piece()
                piece()
                finish(1)
                elu(0)
                elu(1)

            def after_attention(b):
                for half in range(HV):
                    link(dve.scalar_tensor_tensor(out=x1[:, half, :], in0=att[:, half, :], scalar=tanh_gates[:, 0:1],
                                                  in1=x_in[:, half, :], op0=ALU.mult, op1=ALU.add))
                normalise(x1, b, 1)
                if not isinstance(b, int) or b > 0:
                    dve.wait_ge(st_rows, 16 * TOPK * HV * b)
                for half in range(HV):
                    dve.tensor_scalar(rows[0][:, half, 0:D], x1[:, half, :], stats[:, half, 6:7], stats[:, half, 7:8],
                                      ALU.subtract, ALU.mult).then_inc(x_norm_ready, 1)

            def silu_up(n, ready_tanh, ready_silu, ready_hid, s, w, gate, up, dst):
                dve.wait_ge(ready_tanh, n + 1)
                dve.scalar_tensor_tensor(out=gate_silu[:, s, 0:w], in0=gate_tanh[:, s, 0:w], scalar=1.0, in1=gate,
                                         op0=ALU.add, op1=ALU.mult).then_inc(ready_silu, 1)
                dve.wait_ge(ready_silu, n + 1)
                dve.scalar_tensor_tensor(out=dst, in0=gate_silu[:, s, 0:w], scalar=0.5, in1=up,
                                         op0=ALU.mult, op1=ALU.mult).then_inc(ready_hid, 1)

            def shared_piece(c, i, src, s):
                silu_up(PIECES * c + i, tanh_ready, silu_ready, hid_ready, s, N, src[:, 0:N], src[:, N:2 * N],
                        hid_shared[:, i // IC, i % IC, :])

            def save_base(c):
                dve.wait_ge(y_ready, c + 1)
                dve.wait_ge(st_base, 16 * (c + FREE))
                dve.scalar_tensor_tensor(out=y_sb, in0=ps_y.rearrange("p (h d) -> p h d", h=HV), scalar=tanh_gates[:, 1:2],
                                         in1=x1, op0=ALU.mult, op1=ALU.add).then_inc(y_saved, 1)
                dve.wait_ge(y_saved, c + 1)

            def over_experts(ap):
                return ap.rearrange("p (t o) -> p t o", o=1).to_broadcast([P, HV, E])

            def over_tiles(ap, n=HV):
                return ap.rearrange("p (o e) -> p o e", o=1).to_broadcast([P, n, E])

            def te(ap):
                return ap.rearrange("p (t e) -> p t e", e=E)

            def choose(b):
                dve.wait_ge(router_exped, b + 1)
                link(dve.tensor_scalar(score_r, router_exp, 1.0, None, ALU.add))
                link(dve.reciprocal(score_r, score_r))
                for k in range(TOPK):
                    link(dve.tensor_reduce(best[:, k, :], score_r, AX.X, ALU.max))
                    link(dve.tensor_tensor(te(tmp_r), score_r, over_experts(best[:, k, :]), ALU.is_equal))
                    link(dve.tensor_tensor(te(tmp_r), te(tmp_r), over_tiles(ramp_pri), ALU.mult))
                    link(dve.tensor_reduce(top_r, te(tmp_r), AX.X, ALU.max))
                    link(dve.tensor_tensor(te(sel[:, k, :]), te(tmp_r), over_experts(top_r), ALU.is_equal))
                    if k == 0:
                        link(dve.scalar_tensor_tensor(out=score_r, in0=te(sel[:, 0, :]), scalar=-4.0, in1=score_r,
                                                      op0=ALU.mult, op1=ALU.add))
                dve.tensor_tensor(both_bf, sel[:, 0, :], sel[:, 1, :], ALU.add).then_inc(both_ready, 1)

            def place(b):
                link(dve.tensor_tensor(top_r, best[:, 0, :], best[:, 1, :], ALU.add))
                link(dve.reciprocal(top_r, top_r))
                dve.wait_ge(ranks_ready, b + 1)
                link(dve.tensor_tensor(te(before), te(ps_y[:, 0:HV * E]), over_tiles(next_row), ALU.add))
                link(dve.tensor_tensor(next_row, next_row, ps_y[:, HV * E:(HV + 1) * E], ALU.add))
                dve.wait_ge(rows_copied, b + 1)
                for k in range(TOPK):
                    link(dve.tensor_tensor(best[:, k, :], best[:, k, :], top_r, ALU.mult))
                    dve.tensor_scalar(rows[k][:, :, W_COL:W_COL + 1], best[:, k, :].rearrange("p (t o) -> p t o", o=1),
                                      tanh_gates[:, 1:2], None, ALU.mult)
                    dve.tensor_copy(rows[k][:, :, ID_COL:ID_COL + 1].bitcast(I32), token_id.rearrange("p (t o) -> p t o", o=1))
                    link(dve.tensor_tensor(sel[:, k, :], sel[:, k, :], before, ALU.mult))
                    link(dve.tensor_reduce(pos_f[:, k, :], te(sel[:, k, :]), AX.X, ALU.add))
                link(dve.tensor_scalar(token_id, token_id, float(N), None, ALU.add))
                dve.tensor_copy(pos, pos_f).then_inc(sent_ready, 1)

            dve.wait_ge(gates_ready, 1)

            def nothing():
                pass

            start_count(0)
            make_mask(0)

            attention_layer(0, 0, nothing, nothing)
            attention_layer(0, 1, nothing, nothing)
            after_attention(0)
            assert count[0] == DSTEP_FIRST, count[0]
            dve.wait_ge(ramp_ready, RAMPS)
            with dve.Fori(1, B) as b:
                todo = list(range(PIECES))

                def piece():
                    if todo:
                        shared_piece(b - 1, todo.pop(0), ps_gu, 0)

                start_count(DSTEP_GRAPH * b + (DSTEP_FIRST - DSTEP_GRAPH))
                make_mask(b)
                attention_layer(b, 0, piece, lambda: choose(b - 1))
                attention_layer(b, 1, piece, lambda: place(b - 1))
                assert not todo
                save_base(b - 1)
                after_attention(b)
                assert count[0] == DSTEP_GRAPH, count[0]
            start_count(DSTEP_GRAPH * (B - 1) + DSTEP_FIRST)
            choose(B - 1)
            shared_piece(B - 1, 0, ps_chunk[0], 0)
            place(B - 1)
            ev = cmp_r[:, 0:E * TT].rearrange("p (e t) -> p e t", e=E)
            link(dve.tensor_tensor(fill_r, next_row, ramp_region, ALU.subtract))
            link(dve.tensor_tensor(ev, fill_r.rearrange("p (e o) -> p e o", o=1).to_broadcast([P, E, TT]),
                                   ramp_128.rearrange("p (o t) -> p o t", o=1).to_broadcast([P, E, TT]), ALU.is_gt))
            link(dve.tensor_reduce(tiles_r[:, 0, :], ev, AX.X, ALU.add))
            prev = 0
            for shift, at in ((1, 1), (2, 2), (4, 1)):
                v, w = tiles_r[:, prev, :], tiles_r[:, at, :]
                dve.tensor_copy(w[:, 0:shift], v[:, 0:shift])
                link(dve.tensor_tensor(w[:, shift:], v[:, shift:], v[:, 0:E - shift], ALU.add))
                prev = at
            cv = cmp_r.rearrange("p (t e) -> p t e", e=E)
            ramp_over = ramp_tile.rearrange("p (t o) -> p t o", o=1).to_broadcast([P, SLOT_TILES, E])
            link(dve.tensor_tensor(cv, over_tiles(tiles_r[:, prev, :], SLOT_TILES), ramp_over, ALU.is_le))
            link(dve.tensor_reduce(expert_f, cv, AX.X, ALU.add))
            dve.tensor_scalar(expert_i, expert_f, float(E - 1), None, ALU.min)
            link(dve.tensor_tensor(cv, cv, over_tiles(tiles_r[:, 0, :], SLOT_TILES), ALU.mult))
            link(dve.tensor_reduce(start_r, cv, AX.X, ALU.add))
            link(dve.tensor_tensor(start_r, ramp_tile, start_r, ALU.subtract))
            link(dve.tensor_scalar(start_r, start_r, float(P), None, ALU.mult))
            dve.scalar_tensor_tensor(out=row_i, in0=expert_f, scalar=float(REGION), in1=start_r,
                                     op0=ALU.mult, op1=ALU.add).then_inc(table_ready, 1)
            for i in range(1, PIECES):
                shared_piece(B - 1, i, ps_chunk[i % 3], i % 3)
            save_base(B - 1)

            dve.wait_ge(st_base, 16 * (B + FREE))

            def hidden_chunk(q, r, c):
                c0, cw = GATE_CHUNKS[c]
                silu_up(3 * (SLOTS_IN * q + r) + c, r_tanh, r_silu, r_hid, c, cw, ps_chunk[c][:, 0:cw],
                        ps_chunk[c][:, cw:2 * cw], hid[:, r % 2, c0:c0 + cw])

            def scale_output(q, r):
                j = SLOTS_IN * q + r
                dve.wait_ge(r_y, j + 1)
                if not isinstance(j, int) or j >= 2:
                    dve.wait_ge(r_add, 16 * (j - 1))
                dve.tensor_scalar(y_sb[:, r % 2, :], ps_y[:, 0:D], tile_in[:, r % SLOTS_IN, W_COL:W_COL + 1], None, ALU.mult
                                  ).then_inc(r_ysb, 1)

            def step(q, r):
                s = SLOTS_IN * q + r
                inner = not isinstance(s, int)
                if inner or s < SLOT_TILES:
                    hidden_chunk(q, r, 0)
                if inner or s >= 2:
                    scale_output(q, r - 2)
                if inner or s < SLOT_TILES:
                    hidden_chunk(q, r, 1)
                    hidden_chunk(q, r, 2)

            for s in range(PEELED):
                step(0, s)
            with dve.Fori(0, ROUTED_LOOPS) as q:
                for r in range(PEELED, PEELED + SLOTS_IN):
                    step(q, r)
            for s in range(PEELED + SLOTS_IN * ROUTED_LOOPS, SLOT_TILES + 2):
                step(0, s)


def kernel(x, ctx_512, g_xattn, g_ffn, L0_xattn_W0, L0_xattn_a_self0, L0_xattn_a_neigh0, L0_xattn_b0,
           L0_xattn_W1, L0_xattn_a_self1, L0_xattn_a_neigh1, L0_xattn_b1, L0_ffn_w_router, L0_ffn_wg,
           L0_ffn_wu, L0_ffn_wd, L0_ffn_sg, L0_ffn_su, L0_ffn_sd):
    import numpy as np
    import concourse.bacc as bacc
    from concourse import mybir
    from concourse.bass_utils import run_bass_kernel_spmd

    def expert_rows(gate, up, down):
        n = gate.shape[0]
        g = np.asarray(gate).transpose(0, 2, 1).reshape(n, KC, P, I)
        u = np.asarray(up).transpose(0, 2, 1).reshape(n, KC, P, I)
        cols = []
        for c0, cw in GATE_CHUNKS:
            cols += [g[..., c0:c0 + cw], u[..., c0:c0 + cw]]
        gu = np.concatenate(cols, -1).transpose(0, 2, 1, 3).reshape(n, P, KC * GU)
        d = np.asarray(down).transpose(0, 2, 1).reshape(n, IC, P, D).transpose(0, 2, 1, 3).reshape(n, P, IC * D)
        return np.concatenate([gu, d], -1)

    arrays = {
        "x": np.asarray(x).reshape(T, D),
        "ctx_t": np.asarray(ctx_512).transpose(0, 2, 1),
        "w0": np.asarray(L0_xattn_W0).transpose(1, 0, 2).reshape(F_IN, HEADS * FO),
        "w1": np.asarray(L0_xattn_W1).transpose(1, 0, 2).reshape(D, HEADS * FO),
        "params": np.concatenate([np.asarray(a).reshape(-1) for a in (
            L0_xattn_a_self0, L0_xattn_a_neigh0, L0_xattn_a_self1, L0_xattn_a_neigh1,
            L0_xattn_b0, L0_xattn_b1, g_xattn, g_ffn)]),
        "w_router": np.asarray(L0_ffn_w_router).transpose(1, 0),
        "w_experts": np.concatenate([expert_rows(L0_ffn_wg, L0_ffn_wu, L0_ffn_wd),
                                     expert_rows(L0_ffn_sg, L0_ffn_su, L0_ffn_sd)], 0),
    }
    arrays = {n: np.ascontiguousarray(a) for n, a in arrays.items()}
    nc = bacc.Bacc("TRN2", target_bir_lowering=False, num_devices=1)
    args = {n: nc.dram_tensor(n, a.shape, mybir.dt.from_np(a.dtype), kind="ExternalInput").ap()
            for n, a in arrays.items()}
    args["slots"] = nc.dram_tensor("slots", (REGIONS * REGION, ROW), mybir.dt.float32, kind="Internal").ap()
    args["out"] = nc.dram_tensor("out", (T + P, D), mybir.dt.float32, kind="ExternalOutput").ap()
    build(nc, **args)
    r = run_bass_kernel_spmd(nc, [arrays], core_ids=[0])
    return r.results[0]["out"][0:T].reshape(B, N, D)
```

```python
from contextlib import ExitStack

import concourse.bass as bass
from concourse import mybir

F32 = mybir.dt.float32
BF16 = mybir.dt.bfloat16
U32 = mybir.dt.uint32
I32 = mybir.dt.int32
ALU = mybir.AluOpType
ACT = mybir.ActivationFunctionType
AX = mybir.AxisListType

P = 128
B, N, D = 4, 256, 256
F_IN = 64
HEADS, FO = 8, 32
E, NSH, I = 8, 2, 640
T = B * N
HV = N // P
TT = T // P
KC = D // P
IC = I // P
TOPK = 2
SLOT_TILES = TOPK * TT + E - 1
REGION = T + P
REGIONS = E + 1
ROW = D + 8
W_COL, ID_COL = D, D + 1
QUAD = 4
UNITS = HV * HEADS // QUAD
LAYERS = 2
LEAK = 0.2
MASK = 1e10
EPS = 1e-5
BIG = 3.0e38
GU = 2 * I
W_EXP = KC * GU + IC * D
GATE_CHUNKS = ((0, 256), (256, 256), (512, 128))
PARTS = 3
SIDES = 2
PART_ROWS = 32 * PARTS
RAMPS = 12
PIECES = NSH * IC
DOWNS = ((0, 0), (0, 1), (1, 0), (1, 1))
SLOTS_IN = 6
PEELED = 4
ROUTED_LOOPS = (SLOT_TILES - 1 - PEELED) // SLOTS_IN
N_PARAMS = 2 * LAYERS * D + LAYERS * D + 2
ORDER = ((0, 0), (1, 0), (0, 1), (2, 0), (1, 1), (3, 0), (2, 1), (3, 1))
TIGHT = tuple(L for L in range(1, len(ORDER) - 1) if ORDER[L + 1] == (ORDER[L - 1][0], 1))
STREAM = len(ORDER)
ALL_UNITS = STREAM * UNITS
PAIR = 2
FILL_UNITS = 2 * UNITS
FILL_AT = tuple(UNITS * (ORDER.index((n, 1)) + 2) for n in range(PAIR))
ROUTE_AT = (FILL_AT[0] + 6, FILL_AT[1] + 4)
AHEAD = 3


def layers_before(L, layer):
    return sum(1 for n, l in ORDER[:max(L, 0)] if l == layer)


def fill_pieces(w):
    for n, at in enumerate(FILL_AT):
        if at <= w < at + FILL_UNITS:
            return n, (2 * (w - at), 2 * (w - at) + 1)
    return None, ()


def gate_col(i):
    c0, cw = GATE_CHUNKS[i * P // 256]
    return 2 * c0 + i * P - c0, 2 * c0 + cw + i * P - c0


def build(nc, x, ctx_t, w0, w1, params, w_router, w_experts, slots, out):
    with ExitStack() as stack:
        def sb(name, shape, dt=F32):
            return stack.enter_context(nc.sbuf_tensor(name, shape, dt))[(slice(None),) * len(shape)]

        def bank(name, shape, dt=F32):
            return stack.enter_context(nc.psum_tensor(name, shape, dt))[(slice(None),) * len(shape)]

        def sem(name):
            return stack.enter_context(nc.semaphore(name))

        weights = sb("weights", [P, (E + NSH) * W_EXP])
        rows = [[sb(f"rows{c}{k}", [P, HV, ROW]) for k in range(TOPK)] for c in range(PAIR)]
        x_norm_t = [sb(f"x_norm_t{c}", [P, KC, N]) for c in range(PAIR)]
        att_exp = sb("att_exp", [P, HV, D])
        ident = sb("ident", [P, P])
        router_w = sb("router_w", [P, KC, E])
        tanh_gates = sb("tanh_gates", [P, 2])
        hidden = sb("hidden", [P, NSH * IC * N])
        hid_shared = hidden.rearrange("p (e i n) -> p e i n", e=NSH, i=IC)
        hid = hidden[:, 0:2 * I].rearrange("p (s i) -> p s i", s=2)
        hid_t = hidden[:, 2 * I:4 * I].rearrange("p (s i n) -> p s i n", s=2, i=IC)
        gate_tanh = sb("gate_tanh", [P, 3, N])
        gate_silu = sb("gate_silu", [P, 3, N])
        y_sb = sb("y_sb", [P, HV, D])
        tile_in = sb("tile_in", [P, SLOTS_IN, ROW])
        tile_t = sb("tile_t", [P, 2, KC, P])
        w1_sb = sb("w1_sb", [P, KC, D])
        wa_sb = sb("wa_sb", [P, 1 + KC, PART_ROWS])

        LATE = 4
        scratch_at = [(E - LATE) * W_EXP]

        def carve(shape, dt=F32):
            n = 1
            for s in shape[1:]:
                n *= s
            n = n if dt == F32 else (n + 1) // 2
            a = scratch_at[0]
            scratch_at[0] = a + n
            assert scratch_at[0] <= E * W_EXP
            v = weights[:, a:a + n]
            if dt != F32:
                v = v.bitcast(dt)
            if len(shape) == 3:
                v = v.rearrange("p (a b) -> p a b", a=shape[1])
            return v

        x_in = [carve([P, HV, D]) if n < PAIR else sb(f"x_in{n}", [P, HV, D]) for n in range(B)]
        spare_in = tile_in.rearrange("p s r -> p (s r)")
        spare_t = tile_t.rearrange("p s k n -> p (s k n)")
        mask = [carve([P, HV, D]) for n in range(PAIR)] + [
            spare_in[:, n * HV * D:(n + 1) * HV * D].rearrange("p (h d) -> p h d", h=HV) for n in range(B - PAIR)]
        ctx_sb = [carve([P, N]) for c in range(PAIR)]
        w0_sb = carve([P, D])
        params_sb = carve([P, N_PARAMS])
        pick_self = carve([P, HEADS, N], BF16)
        pick_neigh = carve([P, HEADS, P], BF16)
        feat = [carve([P, HV, D]) for c in range(PAIR)]
        parts_t = [carve([P, N], BF16) for c in range(PAIR)]
        rest = carve([P, N])
        logits = carve([P, AHEAD, QUAD * N])
        probs_t = carve([P, 2, QUAD * HV * P])
        neg_max = carve([P, AHEAD, QUAD])
        sums = carve([P, PAIR, HV * HEADS])
        o_inv = carve([P, HV * HEADS])
        stats = [carve([P, HV, 8]) for c in range(PAIR)]
        att = carve([P, HV, D])
        elu = [carve([P, HV, D]) for c in range(PAIR)]
        h0_t = [carve([P, KC, N]) for n in range(PAIR)] + [
            v.rearrange("p (k n) -> p k n", k=KC) for v in (spare_in[:, 2 * HV * D:3 * HV * D], spare_t)]
        wa_prod = att_exp
        a_of = params_sb[:, 0:2 * LAYERS * D].rearrange("p (l s h f) -> p l s h f", l=LAYERS, s=SIDES, h=HEADS)
        bias_of = params_sb[:, 2 * LAYERS * D:3 * LAYERS * D].rearrange("p (l d) -> p l d", l=LAYERS)
        gates = params_sb[:, 3 * LAYERS * D:3 * LAYERS * D + 2]

        ps_z = bank("ps_z", [P, 2, 512])
        ps_pt = bank("ps_pt", [P, QUAD * HV * P])
        ps_y = ps_pt.rearrange("p (h c d) -> p h c d", h=HV, c=PAIR)
        ps_f = bank("ps_f", [P, 512])
        ps_t = bank("ps_t", [P, 512])
        ps_o = bank("ps_o", [P, 512])
        ps_gu = bank("ps_gu", [P, 512])
        ps_chunk = (ps_gu, ps_z[:, 0, :], ps_z[:, 1, :])

        ld_w, ld_w1, ld_params = sem("ld_w"), sem("ld_w1"), sem("ld_params")
        ld_x = [sem(f"ld_x{n}") for n in range(B)]
        ld_ctx = [sem(f"ld_ctx{c}") for c in range(PAIR)]
        ld_shared = sem("ld_shared")
        ld_expert = [sem(f"ld_expert{e}") for e in range(E)]
        const_step, ident_ready = sem("const_step"), sem("ident_ready")
        pick8_ready, pick_ready, ramp_ready = sem("pick8_ready"), sem("pick_ready"), sem("ramp_ready")
        gates_ready, wa_step, wa_ready = sem("gates_ready"), sem("wa_step"), sem("wa_ready")
        dstep, bn_ready, var_ready, inv_ready, mask_ready = sem("dstep"), sem("bn_ready"), sem("var_ready"), sem("inv_ready"), sem("mask_ready")
        pool_passed = sem("pool_passed")
        node_scores, feat_ready, feat_copied, parts_ready = sem("node_scores"), sem("feat_ready"), sem("feat_copied"), sem("parts_ready")
        z_ready, z_copied, bent_ready, max_ready = sem("z_ready"), sem("z_copied"), sem("bent_ready"), sem("max_ready")
        probs_ready, probs_turned = sem("probs_ready"), sem("probs_turned")
        probs_copied = sem("probs_copied")
        o_ready, o_read, att_ready, exp_ready = sem("o_ready"), sem("o_read"), sem("att_ready"), sem("exp_ready")
        h0_ready, h0_turned, h0_copied = sem("h0_ready"), sem("h0_turned"), sem("h0_copied")
        x_norm_ready, x_norm_turned, x_norm_copied = sem("x_norm_ready"), sem("x_norm_turned"), sem("x_norm_copied")
        rows_copied, router_ready, router_exped = sem("rows_copied"), sem("router_ready"), sem("router_exped")
        both_ready, ranks_ready, sent_ready, st_rows = sem("both_ready"), sem("ranks_ready"), sem("sent_ready"), sem("st_rows")
        gu_ready, tanh_ready, silu_ready, hid_ready = sem("gu_ready"), sem("tanh_ready"), sem("silu_ready"), sem("hid_ready")
        y_ready, y_saved, st_base = sem("y_ready"), sem("y_saved"), sem("st_base")
        fill_step, st_fill, table_ready = sem("fill_step"), sem("st_fill"), sem("table_ready")
        r_gu, r_tanh, r_silu, r_hid = sem("r_gu"), sem("r_tanh"), sem("r_silu"), sem("r_hid")
        r_ht, r_htc, r_y, r_ysb = sem("r_ht"), sem("r_htc"), sem("r_y"), sem("r_ysb")
        r_ld = [sem(f"r_ld{i}") for i in range(SLOTS_IN)]
        r_xt, r_xtc, r_add = sem("r_xt"), sem("r_xtc"), sem("r_add")

        w_exp = weights.rearrange("p (e w) -> p e w", e=E + NSH)

        router_exp = sb("router_exp", [P, HV, E])
        score_r = sb("score_r", [P, HV, E])
        sel = sb("sel", [P, TOPK, HV * E])
        both_bf = sb("both_bf", [P, HV * E], BF16)
        tmp_r = sb("tmp_r", [P, HV * E])
        best = sb("best", [P, TOPK, HV])
        top_r = sb("top_r", [P, HV])
        before = sb("before", [P, HV * E])
        next_row = sb("next_row", [P, E])
        pos_f = sb("pos_f", [P, TOPK, HV])
        pos = sb("pos", [P, PAIR, TOPK, HV], U32)
        token_id = sb("token_id", [P, HV])
        fill_r = sb("fill_r", [P, E])
        tiles_r = sb("tiles_r", [P, 3, E])
        cmp_r = sb("cmp_r", [P, SLOT_TILES * E])
        start_r = sb("start_r", [P, SLOT_TILES])
        expert_f = sb("expert_f", [P, SLOT_TILES])
        expert_i = sb("expert_i", [P, SLOT_TILES], I32)
        row_i = sb("row_i", [P, SLOT_TILES], I32)
        ramp_pri = sb("ramp_pri", [P, E])
        ramp_region = sb("ramp_region", [P, E])
        ramp_128 = sb("ramp_128", [P, TT])
        ramp_tile = sb("ramp_tile", [P, SLOT_TILES])
        pick8 = sb("pick8", [P, SIDES, HEADS])
        below = sb("below", [P, P], BF16)
        ones_bf = sb("ones_bf", [P, P], BF16)
        minus_half = sb("minus_half", [P, HV])
        pad_row = sb("pad_row", [P, ROW])
        zero_row = sb("zero_row", [P, D])

        block = stack.enter_context(nc.Block())

        @block.sync
        def _(sp):
            def load_ctx(n):
                sp.dma_start(ctx_sb[n % PAIR][0:F_IN, :], ctx_t[n]).then_inc(ld_ctx[n % PAIR], 16)

            def load_x(n):
                sp.dma_start(x_in[n], x[n * N:(n + 1) * N, :].rearrange("(h p) d -> p h d", p=P)).then_inc(ld_x[n], 16)

            sp.dma_start(params_sb, params.rearrange("(o d) -> o d", o=1).to_broadcast([P, N_PARAMS])).then_inc(ld_params, 16)
            for n in range(PAIR):
                load_ctx(n)
                load_x(n)
            for n in range(PAIR, B):
                load_x(n)
            for n in range(PAIR, B):
                sp.wait_ge(feat_ready, n - PAIR + 1)
                load_ctx(n)
            sp.dma_start(w_exp[:, E:E + NSH, :], w_experts[E:E + NSH].rearrange("e p w -> p e w")).then_inc(ld_shared, 16)
            sp.wait_ge(fill_step, 3)
            fill = pad_row.rearrange("p (o r) -> p o r", o=1).to_broadcast([P, REGION // P, ROW])
            for e in range(REGIONS):
                sp.dma_start(slots[e * REGION:(e + 1) * REGION, :].rearrange("(k p) r -> p k r", p=P), fill).then_inc(st_fill, 16)
            sp.dma_start(out[T:T + P, :], zero_row).then_inc(st_fill, 16)
            for e in range(E - LATE):
                sp.dma_start(w_exp[:, e, :], w_experts[e]).then_inc(ld_expert[e], 16)
            sp.wait_ge(x_norm_ready, HV * B)
            for e in range(E - LATE, E):
                sp.dma_start(w_exp[:, e, :], w_experts[e]).then_inc(ld_expert[e], 16)
            sp.wait_ge(st_rows, 16 * TOPK * TT)
            sp.wait_ge(table_ready, 1)

            def load_tile(j, slot):
                row = sp.value_load(row_i[0:1, bass.ds(j, 1)], min_val=0, max_val=REGION * REGIONS - P)
                sp.dma_start(tile_in[:, slot, :], slots[bass.ds(row, P), :]).then_inc(r_ld[slot], 16)

            for j in range(SLOTS_IN):
                load_tile(j, j)
            FULL = SLOT_TILES // SLOTS_IN - 1
            with sp.Fori(1, 1 + FULL) as q:
                for s in range(SLOTS_IN):
                    j = SLOTS_IN * q + s
                    sp.wait_ge(r_add, 16 * (j - SLOTS_IN + 1))
                    load_tile(j, s)
            for j in range(SLOTS_IN * (1 + FULL), SLOT_TILES):
                sp.wait_ge(r_add, 16 * (j - SLOTS_IN + 1))
                load_tile(j, j % SLOTS_IN)
            sp.wait_ge(r_add, 16 * SLOT_TILES)

        @block.gpsimd
        def _(pool):
            pool.memset(ident, 0.0).then_inc(const_step, 1)
            pool.memset(pick8, 0.0).then_inc(const_step, 1)
            pool.memset(wa_sb, 0.0).then_inc(const_step, 1)
            pool.memset(minus_half, -0.5).then_inc(const_step, 1)
            pool.wait_ge(const_step, 4)
            pool.affine_select(out=ident, in_=ident, compare_op=ALU.not_equal, fill=1.0, base=0,
                               pattern=[[-1, P]], channel_multiplier=1).then_inc(ident_ready, 1)
            for part in range(PARTS):
                if part > 0:
                    pool.wait_ge(pick8_ready, SIDES * part)
                for side in range(SIDES):
                    v = pick8[:, side, :]
                    pool.affine_select(out=v, in_=v, compare_op=ALU.not_equal, fill=1.0,
                                       base=-(32 * part + side * HEADS), pattern=[[-1, HEADS]],
                                       channel_multiplier=1).then_inc(pick8_ready, 1)
            pool.memset(ones_bf, 1.0).then_inc(ramp_ready, 1)
            pool.memset(below, 1.0).then_inc(const_step, 1)
            pool.wait_ge(const_step, 5)
            pool.affine_select(out=below, in_=below, compare_op=ALU.is_gt, fill=0.0, base=0,
                               pattern=[[1, P]], channel_multiplier=-1).then_inc(ramp_ready, 1)
            for ramp, step, first, mult in ((ramp_pri, -1, E, 0), (ramp_128, P, 0, 0), (ramp_tile, 1, 0, 0),
                                            (ramp_region, REGION, 0, 0), (next_row, REGION, 0, 0), (token_id, P, 0, 1)):
                pool.iota(ramp, pattern=[[step, ramp.shape[1]]], base=first, channel_multiplier=mult,
                          allow_small_or_imprecise_dtypes=True).then_inc(ramp_ready, 1)
            pool.memset(zero_row, 0.0).then_inc(fill_step, 1)
            pool.memset(pad_row, 0.0).then_inc(fill_step, 1)
            pool.wait_ge(fill_step, 2)
            pool.iota(pad_row[:, ID_COL:ID_COL + 1].bitcast(I32), pattern=[[0, 1]], base=T,
                      channel_multiplier=1).then_inc(fill_step, 1)
            for c in range(PAIR):
                for k in range(TOPK):
                    pool.memset(rows[c][k][:, :, ID_COL + 1:ROW], 0.0).then_inc(ramp_ready, 1)

            def power(nth, c):
                pool.wait_ge(var_ready, nth + 1)
                pool.tensor_tensor(stats[c][:, :, 7:8], stats[c][:, :, 7:8], minus_half.rearrange("p (a o) -> p a o", o=1),
                                   ALU.pow).then_inc(inv_ready, 1)

            def copy_rows(n, c):
                pool.wait_ge(x_norm_ready, HV * n + HV)
                pool.sem_inc(pool_passed, 1)
                pool.tensor_copy(rows[c][1][:, :, 0:D], rows[c][0][:, :, 0:D]).then_inc(rows_copied, 1)

            def send_rows(n, c):
                pool.wait_ge(sent_ready, n + 1)
                pool.sem_inc(pool_passed, 1)
                for k in range(TOPK):
                    for half in range(HV):
                        pool.indirect_dma_start(
                            out=slots, out_offset=bass.IndirectOffsetOnAxis(ap=pos[:, c, k, half:half + 1], axis=0),
                            in_=rows[c][k][:, half, :], in_offset=None).then_inc(st_rows, 16)

            for n in range(B):
                power(n, n % PAIR)
            for n in range(B):
                power(B + n, n % PAIR)
                copy_rows(n, n % PAIR)
                if n == 1:
                    pool.wait_ge(st_fill, 16 * (REGIONS + 1))
                if n >= 1:
                    send_rows(n - 1, (n - 1) % PAIR)
            send_rows(B - 1, (B - 1) % PAIR)
            pool.wait_ge(st_base, 16 * B)

            def add_tile(j, slot, y_slot):
                pool.wait_ge(r_ysb, j + 1)
                pool.sem_inc(pool_passed, 1)
                pool.indirect_dma_start(
                    out=out, out_offset=bass.IndirectOffsetOnAxis(ap=tile_in[:, slot, ID_COL:ID_COL + 1].bitcast(U32), axis=0),
                    in_=y_sb[:, y_slot, :], in_offset=None, compute_op=ALU.add).then_inc(r_add, 16)
                pool.wait_ge(r_add, 16 * (j + 1))

            with pool.Fori(0, SLOT_TILES // SLOTS_IN) as q:
                for s in range(SLOTS_IN):
                    add_tile(SLOTS_IN * q + s, s, s % 2)
            for j in range(SLOT_TILES - SLOT_TILES % SLOTS_IN, SLOT_TILES):
                add_tile(j, j % SLOTS_IN, j % 2)

        @block.tensor
        def _(pe):
            def features(L):
                n, layer = ORDER[L]
                if layer == 0:
                    pe.wait_ge(ld_ctx[n % PAIR], 16 * (n // PAIR + 1))
                    v = ctx_sb[n % PAIR]
                    src = [(v[0:F_IN, :], w0_sb[0:F_IN, :], wa_sb[0:F_IN, 0, :])]
                else:
                    pe.wait_ge(wa_ready, 2)
                    pe.wait_ge(ld_w1, 16)
                    pe.wait_ge(h0_copied, n + 1)
                    src = [(h0_t[n][:, k, :], w1_sb[:, k, :], wa_sb[:, 1 + k, :]) for k in range(KC)]
                for k, (v, w, wa) in enumerate(src):
                    mm = pe.matmul(ps_t[0:PART_ROWS, 0:N], wa, v, start=(k == 0), stop=(k == len(src) - 1))
                mm.then_inc(node_scores, 1)
                if L > 0:
                    pe.wait_ge(feat_copied, L)
                if L == STREAM - 1:
                    pe.wait_ge(router_exped, 1)
                    pe.wait_ge(sent_ready, 1)
                for half in range(HV):
                    for k, (v, w, wa) in enumerate(src):
                        mm = pe.matmul(ps_f[:, half * D:(half + 1) * D], v[:, half * P:(half + 1) * P], w,
                                       start=(k == 0), stop=(k == len(src) - 1))
                mm.then_inc(feat_ready, 1)

            def scores(w):
                L, u = w // UNITS, w % UNITS
                half, quad = u // 2, u % 2
                v = parts_t[L % PAIR]
                if u == 0:
                    pe.wait_ge(parts_ready, L + 1)
                if w > 0:
                    pe.wait_ge(z_copied, w)
                for pair in range(QUAD // 2):
                    h = quad * QUAD + 2 * pair
                    pe.matmul(ps_z[:, pair, :], v[0:PART_ROWS, half * P:(half + 1) * P],
                              pick_self[0:PART_ROWS, h:h + 2, :], start=True, stop=False, skip_group_check=True)
                    for i in range(2):
                        mm = pe.matmul(ps_z[:, pair, i * N:(i + 1) * N], pick_neigh[0:PART_ROWS, h + i, :],
                                       v[0:PART_ROWS, :], start=False, stop=True, skip_group_check=True)
                mm.then_inc(z_ready, 1)

            def turn(w):
                pe.wait_ge(probs_ready, w + 1)
                if w > 0:
                    pe.wait_ge(probs_copied, w)
                for i in range(QUAD * HV):
                    mm = pe.transpose(ps_pt[:, i * P:(i + 1) * P], logits[:, w % AHEAD, i * P:(i + 1) * P], ident)
                mm.then_inc(probs_turned, 1)

            def weigh(w):
                L, u = w // UNITS, w % UNITS
                half, quad = u // 2, u % 2
                if u == 0:
                    pe.wait_ge(feat_copied, L + 1)
                    if L > 0:
                        pe.wait_ge(o_read, L)
                pe.wait_ge(probs_copied, w + 1)
                for i in range(QUAD):
                    h = quad * QUAD + i
                    for m in range(HV):
                        mm = pe.matmul(ps_o[:, half * D + h * FO:half * D + (h + 1) * FO],
                                       probs_t[:, w % 2, (i * HV + m) * P:(i * HV + m + 1) * P],
                                       feat[L % PAIR][:, m, h * FO:(h + 1) * FO],
                                       start=(m == 0), stop=(m == HV - 1))
                if u == UNITS - 1:
                    mm.then_inc(o_ready, 1)

            def turn_rows(src, done):
                for half in range(HV):
                    for k in range(KC):
                        mm = pe.transpose(ps_t[:, (k * HV + half) * P:(k * HV + half + 1) * P],
                                          src[:, half, k * P:(k + 1) * P], ident)
                mm.then_inc(done, 1)

            def turn_h0(n):
                pe.wait_ge(h0_ready, n + 1)
                turn_rows(elu[ORDER.index((n, 0)) % PAIR], h0_turned)

            def turn_x_norm(n):
                pe.wait_ge(x_norm_ready, HV * (n + 1))
                turn_rows(rows[n % PAIR][0], x_norm_turned)

            def router(n):
                pe.wait_ge(x_norm_copied, n + 1)
                if n > 0:
                    pe.wait_ge(router_exped, n)
                for half in range(HV):
                    for k in range(KC):
                        mm = pe.matmul(ps_f[:, half * E:(half + 1) * E], x_norm_t[n % PAIR][:, k, half * P:(half + 1) * P],
                                       router_w[:, k, :], start=(k == 0), stop=(k == KC - 1))
                mm.then_inc(router_ready, 1)

            def ranks(n, dst):
                pe.wait_ge(both_ready, n + 1)
                first, second = both_bf[:, 0:E], both_bf[:, E:2 * E]
                pe.matmul(dst[:, 0:E], below, first, start=True, stop=True)
                pe.matmul(dst[:, E:2 * E], below, second, start=True, stop=False)
                pe.matmul(dst[:, E:2 * E], ones_bf, first, start=False, stop=True)
                pe.matmul(dst[:, 2 * E:3 * E], ones_bf, first, start=True, stop=False)
                pe.matmul(dst[:, 2 * E:3 * E], ones_bf, second, start=False, stop=True).then_inc(ranks_ready, 1)

            def gate_up(n, i, dst):
                base = (E + i // IC) * W_EXP
                for part, col in enumerate(gate_col(i % IC)):
                    for k in range(KC):
                        a = base + k * GU + col
                        mm = pe.matmul(dst[:, part * N:(part + 1) * N], weights[:, a:a + P],
                                       x_norm_t[n % PAIR][:, k, :], start=(k == 0), stop=(k == KC - 1))
                mm.then_inc(gu_ready, 1)

            def down(n, half, e, dst):
                for i in range(IC):
                    a = (E + e) * W_EXP + KC * GU + i * D
                    mm = pe.matmul(dst, hid_shared[:, e, i, half * P:(half + 1) * P], weights[:, a:a + D],
                                   start=(e == 0 and i == 0), stop=(e == NSH - 1 and i == IC - 1))
                if half == HV - 1 and e == NSH - 1:
                    mm.then_inc(y_ready, 1)

            def filler(n, piece):
                if piece == 0:
                    pe.wait_ge(x_norm_copied, n + 1)
                    if n > 0:
                        pe.wait_ge(y_saved, n)
                if piece < PIECES:
                    if piece > 0:
                        pe.wait_ge(hid_ready, PIECES * n + piece)
                    gate_up(n, piece, ps_gu)
                elif piece < PIECES + len(DOWNS):
                    half, e = DOWNS[piece - PIECES]
                    if piece == PIECES:
                        pe.wait_ge(hid_ready, PIECES * (n + 1))
                    down(n, half, e, ps_gu[:, half * D:(half + 1) * D])

            pe.wait_ge(ident_ready, 1)
            pe.wait_ge(ld_w, 32)
            pe.wait_ge(wa_ready, 1)
            pe.wait_ge(pick_ready, 2)
            features(0)
            scores(0)
            features(1)
            scores(1)
            for w in range(ALL_UNITS):
                L, u = w // UNITS, w % UNITS
                filled, pieces = fill_pieces(w)
                if filled == 0:
                    pe.wait_ge(ld_shared, 16)
                tight = L in TIGHT and u == 2
                after_tight = L in TIGHT and u == 3
                if w in ROUTE_AT:
                    pe.wait_ge(feat_copied, min(L + 2, STREAM))
                    router(filled)
                if tight:
                    turn_h0(ORDER[L - 1][0])
                elif w + 2 < ALL_UNITS and not after_tight:
                    scores(w + 2)
                turn(w)
                if after_tight:
                    scores(w + 2)
                if u == 0 and 0 < L < STREAM - 1 and L not in TIGHT:
                    pe.wait_ge(h0_copied, layers_before(L - 1, 0))
                    if L - 1 > 2:
                        pe.wait_ge(x_norm_copied, layers_before(L - 1, 1))
                    features(L + 1)
                if u == 3 and L > 0 and L not in TIGHT and ORDER[L - 1][1] == 0:
                    turn_h0(ORDER[L - 1][0])
                if pieces:
                    filler(filled, pieces[0])
                if tight:
                    features(L + 1)
                if w > 0:
                    weigh(w - 1)
                if u == 3 and L > 0 and ORDER[L - 1][1] == 1:
                    turn_x_norm(ORDER[L - 1][0])
                if pieces:
                    filler(filled, pieces[1])
                if tight:
                    scores(w + 2)
                if w - 1 in ROUTE_AT:
                    ranks(filled, ps_f)
            for n in range(PAIR, B):
                for i in range(PIECES):
                    m = PIECES * (n - PAIR) + i
                    if m == 0:
                        pe.wait_ge(x_norm_copied, n + 1)
                        pe.wait_ge(y_saved, n)
                    if m == 1:
                        pe.wait_ge(z_copied, ALL_UNITS)
                    if m >= 3:
                        pe.wait_ge(hid_ready, PIECES * n + i - 2)
                    gate_up(n, i, ps_chunk[m % 3])
                    if m == 0:
                        weigh(ALL_UNITS - 1)
                    if m == 1:
                        pe.wait_ge(sent_ready, n)
                        router(n)
                    if i == 6:
                        if n == PAIR:
                            pe.wait_ge(o_read, STREAM)
                        ranks(n, ps_o)
                if n + 1 < B:
                    turn_x_norm(n + 1)
                for e in range(NSH):
                    pe.wait_ge(hid_ready, PIECES * n + IC * (e + 1))
                    if n > PAIR and e == 0:
                        pe.wait_ge(y_saved, n)
                    for half in range(HV):
                        down(n, half, e, ps_y[:, half, n % PAIR, :])
                    if e == 0 and n + 1 < B:
                        router(n + 1)

            for e in range(E):
                pe.wait_ge(ld_expert[e], 16)

            def turn_in(q, r):
                j = SLOTS_IN * q + r
                pe.wait_ge(r_ld[r % SLOTS_IN], 16 * (q + r // SLOTS_IN + 1))
                if not isinstance(j, int) or j >= 1:
                    pe.wait_ge(r_xtc, j)
                for k in range(KC):
                    mm = pe.transpose(ps_t[:, k * P:(k + 1) * P], tile_in[:, r % SLOTS_IN, k * P:(k + 1) * P], ident)
                mm.then_inc(r_xt, 1)

            def gate_chunk(q, r, c, off):
                j = SLOTS_IN * q + r
                c0, cw = GATE_CHUNKS[c]
                if c == 0:
                    pe.wait_ge(r_xtc, j + 1)
                if not isinstance(j, int) or j >= 1:
                    pe.wait_ge(r_hid, 3 * j + c - 2)
                for k in range(KC):
                    mm = pe.matmul(ps_chunk[c][:, 0:2 * cw], tile_t[:, r % 2, k, :],
                                   weights[:, bass.ds(off + (k * GU + 2 * c0), 2 * cw)],
                                   start=(k == 0), stop=(k == KC - 1))
                mm.then_inc(r_gu, 1)

            def expert_at(q, r):
                e = pe.value_load(expert_i[0:1, bass.ds(SLOTS_IN * q + r, 1)], min_val=0, max_val=E - 1)
                return e * W_EXP

            def turn_hidden(q, r):
                j = SLOTS_IN * q + r
                pe.wait_ge(r_hid, 3 * j + 3)
                if not isinstance(j, int) or j >= 1:
                    pe.wait_ge(r_htc, j)
                for i in range(IC):
                    mm = pe.transpose(ps_pt[:, i * P:(i + 1) * P], hid[:, r % 2, i * P:(i + 1) * P], ident)
                mm.then_inc(r_ht, 1)

            def down_tile(q, r):
                j = SLOTS_IN * q + r
                off = expert_at(q, r)
                pe.wait_ge(r_htc, j + 1)
                if not isinstance(j, int) or j >= 1:
                    pe.wait_ge(r_ysb, j)
                for i in range(IC):
                    mm = pe.matmul(ps_o[:, 0:D], hid_t[:, r % 2, i, :],
                                   weights[:, bass.ds(off + (KC * GU + i * D), D)], start=(i == 0), stop=(i == IC - 1))
                mm.then_inc(r_y, 1)

            def step(q, r):
                s = SLOTS_IN * q + r
                inner = not isinstance(s, int)
                off = expert_at(q, r) if inner or s < SLOT_TILES else None
                if off is not None:
                    gate_chunk(q, r, 0, off)
                if inner or s >= 2:
                    down_tile(q, r - 2)
                if off is not None:
                    gate_chunk(q, r, 1, off)
                    gate_chunk(q, r, 2, off)
                if inner or s + 1 < SLOT_TILES:
                    turn_in(q, r + 1)
                if inner or 1 <= s <= SLOT_TILES:
                    turn_hidden(q, r - 1)

            pe.wait_ge(table_ready, 1)
            pe.wait_ge(y_saved, B)
            turn_in(0, 0)
            for s in range(PEELED):
                step(0, s)
            with pe.Fori(0, ROUTED_LOOPS) as q:
                for r in range(PEELED, PEELED + SLOTS_IN):
                    step(q, r)
            for s in range(PEELED + SLOTS_IN * ROUTED_LOOPS, SLOT_TILES + 2):
                step(0, s)

        @block.scalar
        def _(act):
            act.dma_start(w0_sb[0:F_IN, :], w0).then_inc(ld_w, 16)
            act.dma_start(w1_sb, w1.rearrange("(k p) n -> p k n", p=P)).then_inc(ld_w1, 16)
            act.dma_start(router_w, w_router.rearrange("(k p) e -> p k e", p=P)).then_inc(ld_w, 16)
            act.wait_ge(ld_params, 16)
            act.activation(tanh_gates, gates, ACT.Tanh).then_inc(gates_ready, 1)

            act.wait_ge(pick8_ready, SIDES * PARTS)
            act.activation(pick_self, pick8[:, 0, :].rearrange("p (h o) -> p h o", o=1).to_broadcast([P, HEADS, N]),
                           ACT.Copy).then_inc(pick_ready, 1)
            act.activation(pick_neigh, pick8[:, 1, :].rearrange("p (h o) -> p h o", o=1).to_broadcast([P, HEADS, P]),
                           ACT.Copy).then_inc(pick_ready, 1)

            def copy_features(L):
                act.wait_ge(feat_ready, L + 1)
                if L >= PAIR:
                    act.wait_ge(o_ready, L - PAIR + 1)
                act.activation(feat[L % PAIR].rearrange("p a d -> p (a d)"), ps_f, ACT.Copy).then_inc(feat_copied, 1)

            def copy_scores(w):
                act.wait_ge(z_ready, w + 1)
                act.activation(logits[:, w % AHEAD, :], ps_z.rearrange("p a n -> p (a n)"), ACT.Copy).then_inc(z_copied, 1)

            def exponent(w):
                L, u = w // UNITS, w % UNITS
                act.wait_ge(max_ready, w + 1)
                for i in range(QUAD):
                    v = logits[:, w % AHEAD, i * N:(i + 1) * N]
                    s = u * QUAD + i
                    ins = act.activation(v, v, ACT.Exp, bias=neg_max[:, w % AHEAD, i:i + 1], scale=-1.0,
                                         accum_out=sums[:, L % PAIR, s:s + 1])
                ins.then_inc(probs_ready, 1)

            def copy_turned(w):
                act.wait_ge(probs_turned, w + 1)
                act.activation(probs_t[:, w % 2, :], ps_pt, ACT.Copy).then_inc(probs_copied, 1)

            def elu_exponent(L):
                act.wait_ge(att_ready, L + 1)
                act.activation(att_exp, att, ACT.Exp).then_inc(exp_ready, 1)

            def copy_h0(n):
                act.wait_ge(h0_turned, n + 1)
                act.activation(h0_t[n].rearrange("p k n -> p (k n)"), ps_t, ACT.Copy).then_inc(h0_copied, 1)

            def copy_x_norm(n):
                act.wait_ge(x_norm_turned, n + 1)
                act.activation(x_norm_t[n % PAIR].rearrange("p k n -> p (k n)"), ps_t, ACT.Copy).then_inc(x_norm_copied, 1)

            def router_exponent(n):
                act.wait_ge(router_ready, n + 1)
                if n > 0:
                    act.wait_ge(both_ready, n)
                act.activation(router_exp, ps_f[:, 0:HV * E].rearrange("p (a e) -> p a e", a=HV), ACT.Exp, scale=-1.0).then_inc(router_exped, 1)

            def tanh_piece(n, i, s):
                act.wait_ge(gu_ready, PIECES * n + i + 1)
                act.activation(gate_tanh[:, s, :], ps_chunk[s][:, 0:N], ACT.Tanh, scale=0.5).then_inc(tanh_ready, 1)

            def store_base(n):
                act.wait_ge(y_saved, n + 1)
                act.dma_start(out[n * N:(n + 1) * N, :].rearrange("(h p) d -> p h d", p=P), y_sb).then_inc(st_base, 16)

            copy_features(0)
            copy_scores(0)
            copy_features(1)
            copy_scores(1)
            exponent(0)
            for w in range(ALL_UNITS):
                L, u = w // UNITS, w % UNITS
                filled, pieces = fill_pieces(w)
                tight = L in TIGHT and u == 2
                if w in ROUTE_AT:
                    router_exponent(filled)
                if w + 2 < ALL_UNITS and not tight:
                    copy_scores(w + 2)
                if not pieces:
                    copy_turned(w)
                if u == 1 and L in TIGHT:
                    elu_exponent(L - 1)
                if w + 1 < ALL_UNITS:
                    exponent(w + 1)
                if u == 1 and L >= 1 and L not in TIGHT:
                    elu_exponent(L - 1)
                if pieces and pieces[0] < PIECES:
                    tanh_piece(filled, pieces[0], 0)
                if pieces:
                    copy_turned(w)
                if u == 1 and 0 < L < STREAM - 1 and L not in TIGHT:
                    copy_features(L + 1)
                if u == 3 and L > 0 and L not in TIGHT and ORDER[L - 1][1] == 0:
                    copy_h0(ORDER[L - 1][0])
                if tight:
                    copy_features(L + 1)
                if u == 3 and L > 0 and ORDER[L - 1][1] == 1:
                    copy_x_norm(ORDER[L - 1][0])
                if pieces and pieces[0] < PIECES:
                    tanh_piece(filled, pieces[1], 0)
                if tight:
                    copy_scores(w + 2)
                if u == 1 and L in TIGHT:
                    copy_h0(ORDER[L - 1][0])
                if w - (FILL_UNITS - 1) in FILL_AT:
                    store_base(filled)
            for n in range(PAIR, B):
                for i in range(PIECES):
                    tanh_piece(n, i, (PIECES * (n - PAIR) + i) % 3)
                    if n == PAIR and i == 0:
                        elu_exponent(STREAM - 1)
                    if n == PAIR and i == 2:
                        router_exponent(n)
                if n + 1 < B:
                    copy_x_norm(n + 1)
                    router_exponent(n + 1)
                store_base(n)

            def copy_in(q, r):
                act.wait_ge(r_xt, SLOTS_IN * q + r + 1)
                act.activation(tile_t[:, r % 2, :, :].rearrange("p a b -> p (a b)"), ps_t[:, 0:D], ACT.Copy).then_inc(r_xtc, 1)

            def step(q, r):
                s = SLOTS_IN * q + r
                inner = not isinstance(s, int)
                if inner or s < SLOT_TILES:
                    for c, (c0, cw) in enumerate(GATE_CHUNKS):
                        act.wait_ge(r_gu, 3 * s + c + 1)
                        act.activation(gate_tanh[:, c, 0:cw], ps_chunk[c][:, 0:cw], ACT.Tanh, scale=0.5).then_inc(r_tanh, 1)
                if inner or s + 1 < SLOT_TILES:
                    copy_in(q, r + 1)
                if inner or s >= 1:
                    act.wait_ge(r_ht, s)
                    act.activation(hid_t[:, (r - 1) % 2, :, :].rearrange("p a b -> p (a b)"), ps_pt[:, 0:I], ACT.Copy
                                   ).then_inc(r_htc, 1)

            copy_in(0, 0)
            for s in range(PEELED):
                step(0, s)
            with act.Fori(0, ROUTED_LOOPS) as q:
                for r in range(PEELED, PEELED + SLOTS_IN):
                    step(q, r)
            for s in range(PEELED + SLOTS_IN * ROUTED_LOOPS, SLOT_TILES + 1):
                step(0, s)

        @block.vector
        def _(dve):
            count = [0]

            def link(ins):
                count[0] += 1
                ins.then_inc(dstep, 1)
                dve.wait_ge(dstep, count[0])

            dve.wait_ge(ld_params, 16)
            dve.wait_ge(ld_w, 32)
            dve.wait_ge(const_step, 4)
            n_wa = 0
            for layer, k, w, np_ in ((0, 0, w0_sb, F_IN), (1, 1, w1_sb[:, 0, :], P), (1, 2, w1_sb[:, 1, :], P)):
                if k == 1:
                    dve.wait_ge(ld_w1, 16)
                prod = wa_prod.rearrange("p a b -> p (a b)")[0:np_, :]
                dve.tensor_tensor(prod.rearrange("p (s h f) -> p s h f", s=SIDES, h=HEADS),
                                  w[0:np_, :].rearrange("p (s h f) -> p s h f", s=1, h=HEADS).to_broadcast([np_, SIDES, HEADS, FO]),
                                  a_of[0:np_, layer], ALU.mult).then_inc(wa_step, 1)
                n_wa += 1
                dve.wait_ge(wa_step, n_wa)
                ins = dve.tensor_reduce(wa_sb[0:np_, k, 0:SIDES * HEADS], prod.rearrange("p (s f) -> p s f", f=FO), AX.X, ALU.add)
                ins.then_inc(wa_step, 1)
                n_wa += 1
                dve.wait_ge(wa_step, n_wa)
                for part in range(1, PARTS):
                    ins = dve.tensor_copy(wa_sb[0:np_, k, 32 * part:32 * part + SIDES * HEADS], wa_sb[0:np_, k, 0:SIDES * HEADS])
                if k != 1:
                    ins.then_inc(wa_ready, 1)

            def normalise(src, c, nth):
                for half in range(HV):
                    dve.bn_stats(stats[c][:, half, 0:6], src[:, half, :]).then_inc(bn_ready, 1)
                dve.wait_ge(bn_ready, HV * (nth + 1))
                for half in range(HV):
                    ins = dve.bn_aggr(stats[c][:, half, 6:8], stats[c][:, half, 0:6])
                link(ins)
                dve.tensor_scalar(stats[c][:, :, 7:8], stats[c][:, :, 7:8], EPS, None, ALU.add).then_inc(var_ready, 1)
                dve.wait_ge(inv_ready, nth + 1)

            def make_mask(n):
                c = n % PAIR
                dve.wait_ge(ld_x[n], 16)
                normalise(x_in[n], c, n)
                for half in range(HV):
                    ins = dve.tensor_scalar(mask[n][:, half, :], x_in[n][:, half, :], stats[c][:, half, 6:7], stats[c][:, half, 7:8],
                                            ALU.subtract, ALU.mult)
                link(ins)
                dve.tensor_scalar(mask[n], mask[n], 1.0, MASK, ALU.subtract, ALU.mult).then_inc(mask_ready, 1)

            def split_scores(L):
                dve.wait_ge(node_scores, L + 1)
                v, z = parts_t[L % PAIR], ps_t[0:PART_ROWS, 0:N]
                link(dve.tensor_copy(v[0:PART_ROWS, :], z))
                link(dve.tensor_tensor(rest[0:PART_ROWS, :], z, v[0:PART_ROWS, :], ALU.subtract))
                link(dve.tensor_copy(v[0:64, :], rest[0:64, :]))
                dve.tensor_tensor(v[0:32, :], rest[0:32, :], v[0:32, :], ALU.subtract).then_inc(parts_ready, 1)

            def mask_max(w):
                L, u = w // UNITS, w % UNITS
                n, layer = ORDER[L]
                if u == 0 and layer == 0:
                    dve.wait_ge(mask_ready, n + 1)
                dve.wait_ge(z_copied, w + 1)
                z = logits[:, w % AHEAD, :]
                dve.scalar_tensor_tensor(out=z, in0=z, scalar=LEAK, in1=z, op0=ALU.mult, op1=ALU.max).then_inc(bent_ready, 1)
                dve.wait_ge(bent_ready, w + 1)
                for i in range(QUAD):
                    v = logits[:, w % AHEAD, i * N:(i + 1) * N]
                    ins = dve.tensor_tensor_reduce(v, v, mask[n][:, u // 2, :], -1.0, BIG, ALU.add, ALU.min,
                                                   neg_max[:, w % AHEAD, i:i + 1])
                ins.then_inc(max_ready, 1)

            def divide(L):
                c = L % PAIR
                dve.wait_ge(o_ready, L + 1)
                link(dve.reciprocal(o_inv, sums[:, c, :]))
                dve.tensor_tensor(att.rearrange("p a (h f) -> p (a h) f", h=HEADS), ps_o.rearrange("p (h f) -> p h f", f=FO),
                                  o_inv.rearrange("p (h o) -> p h o", o=1).to_broadcast([P, HV * HEADS, FO]), ALU.mult
                                  ).then_inc(o_read, 1)
                dve.wait_ge(o_read, L + 1)
                dve.tensor_tensor(att, att, bias_of[:, ORDER[L][1], :].rearrange("p (o d) -> p o d", o=1).to_broadcast([P, HV, D]),
                                  ALU.add).then_inc(att_ready, 1)
                dve.wait_ge(att_ready, L + 1)
                link(dve.tensor_scalar(elu[c], att, 0.0, -1.0, ALU.max, ALU.add))

            def end_elu(L):
                c = L % PAIR
                dve.wait_ge(exp_ready, L + 1)
                ins = dve.scalar_tensor_tensor(out=elu[c], in0=att_exp, scalar=1.0, in1=elu[c], op0=ALU.min, op1=ALU.add)
                if ORDER[L][1] == 0:
                    ins.then_inc(h0_ready, 1)
                else:
                    link(ins)

            def after_attention(n):
                c = n % PAIR
                link(dve.scalar_tensor_tensor(out=x_in[n], in0=elu[ORDER.index((n, 1)) % PAIR], scalar=tanh_gates[:, 0:1], in1=x_in[n],
                                              op0=ALU.mult, op1=ALU.add))
                normalise(x_in[n], c, B + n)
                if n >= PAIR:
                    dve.wait_ge(st_rows, 16 * TOPK * HV * (n - PAIR + 1))
                for half in range(HV):
                    dve.tensor_scalar(rows[c][0][:, half, 0:D], x_in[n][:, half, :], stats[c][:, half, 6:7], stats[c][:, half, 7:8],
                                      ALU.subtract, ALU.mult).then_inc(x_norm_ready, 1)

            def silu_up(n, ready_tanh, ready_silu, ready_hid, s, w, gate, up, dst):
                dve.wait_ge(ready_tanh, n + 1)
                dve.scalar_tensor_tensor(out=gate_silu[:, s, 0:w], in0=gate_tanh[:, s, 0:w], scalar=1.0, in1=gate,
                                         op0=ALU.add, op1=ALU.mult).then_inc(ready_silu, 1)
                dve.wait_ge(ready_silu, n + 1)
                dve.scalar_tensor_tensor(out=dst, in0=gate_silu[:, s, 0:w], scalar=0.5, in1=up,
                                         op0=ALU.mult, op1=ALU.mult).then_inc(ready_hid, 1)

            def shared_piece(n, i, s):
                silu_up(PIECES * n + i, tanh_ready, silu_ready, hid_ready, s, N, ps_chunk[s][:, 0:N],
                        ps_chunk[s][:, N:2 * N], hid_shared[:, i // IC, i % IC, :])

            def save_base(n, src):
                dve.wait_ge(y_ready, n + 1)
                if n > 0:
                    dve.wait_ge(st_base, 16 * n)
                dve.scalar_tensor_tensor(out=y_sb, in0=src, scalar=tanh_gates[:, 1:2], in1=x_in[n],
                                         op0=ALU.mult, op1=ALU.add).then_inc(y_saved, 1)

            def over_experts(ap):
                return ap.rearrange("p (t o) -> p t o", o=1).to_broadcast([P, HV, E])

            def over_tiles(ap, n=HV):
                return ap.rearrange("p (o e) -> p o e", o=1).to_broadcast([P, n, E])

            def te(ap):
                return ap.rearrange("p (t e) -> p t e", e=E)

            def choose(n):
                dve.wait_ge(router_exped, n + 1)
                link(dve.tensor_scalar(score_r, router_exp, 1.0, None, ALU.add))
                link(dve.reciprocal(score_r, score_r))
                for k in range(TOPK):
                    link(dve.tensor_reduce(best[:, k, :], score_r, AX.X, ALU.max))
                    link(dve.tensor_tensor(te(tmp_r), score_r, over_experts(best[:, k, :]), ALU.is_equal))
                    link(dve.tensor_tensor(te(tmp_r), te(tmp_r), over_tiles(ramp_pri), ALU.mult))
                    link(dve.tensor_reduce(top_r, te(tmp_r), AX.X, ALU.max))
                    link(dve.tensor_tensor(te(sel[:, k, :]), te(tmp_r), over_experts(top_r), ALU.is_equal))
                    if k == 0:
                        link(dve.scalar_tensor_tensor(out=score_r, in0=te(sel[:, 0, :]), scalar=-4.0, in1=score_r,
                                                      op0=ALU.mult, op1=ALU.add))
                dve.tensor_tensor(both_bf, sel[:, 0, :], sel[:, 1, :], ALU.add).then_inc(both_ready, 1)

            def place(n, src):
                c = n % PAIR
                link(dve.tensor_tensor(top_r, best[:, 0, :], best[:, 1, :], ALU.add))
                link(dve.reciprocal(top_r, top_r))
                dve.wait_ge(ranks_ready, n + 1)
                link(dve.tensor_tensor(te(before), te(src[:, 0:HV * E]), over_tiles(next_row), ALU.add))
                link(dve.tensor_tensor(next_row, next_row, src[:, HV * E:(HV + 1) * E], ALU.add))
                dve.wait_ge(rows_copied, n + 1)
                for k in range(TOPK):
                    link(dve.tensor_tensor(best[:, k, :], best[:, k, :], top_r, ALU.mult))
                    dve.tensor_scalar(rows[c][k][:, :, W_COL:W_COL + 1], best[:, k, :].rearrange("p (t o) -> p t o", o=1),
                                      tanh_gates[:, 1:2], None, ALU.mult)
                    dve.tensor_copy(rows[c][k][:, :, ID_COL:ID_COL + 1].bitcast(I32), token_id.rearrange("p (t o) -> p t o", o=1))
                    link(dve.tensor_tensor(sel[:, k, :], sel[:, k, :], before, ALU.mult))
                    link(dve.tensor_reduce(pos_f[:, k, :], te(sel[:, k, :]), AX.X, ALU.add))
                link(dve.tensor_scalar(token_id, token_id, float(N), None, ALU.add))
                dve.tensor_copy(pos[:, c, :, :], pos_f).then_inc(sent_ready, 1)

            def make_table():
                ev = cmp_r[:, 0:E * TT].rearrange("p (e t) -> p e t", e=E)
                link(dve.tensor_tensor(fill_r, next_row, ramp_region, ALU.subtract))
                link(dve.tensor_tensor(ev, fill_r.rearrange("p (e o) -> p e o", o=1).to_broadcast([P, E, TT]),
                                       ramp_128.rearrange("p (o t) -> p o t", o=1).to_broadcast([P, E, TT]), ALU.is_gt))
                link(dve.tensor_reduce(tiles_r[:, 0, :], ev, AX.X, ALU.add))
                prev = 0
                for shift, at in ((1, 1), (2, 2), (4, 1)):
                    v, w = tiles_r[:, prev, :], tiles_r[:, at, :]
                    dve.tensor_copy(w[:, 0:shift], v[:, 0:shift])
                    link(dve.tensor_tensor(w[:, shift:], v[:, shift:], v[:, 0:E - shift], ALU.add))
                    prev = at
                cv = cmp_r.rearrange("p (t e) -> p t e", e=E)
                ramp_over = ramp_tile.rearrange("p (t o) -> p t o", o=1).to_broadcast([P, SLOT_TILES, E])
                link(dve.tensor_tensor(cv, over_tiles(tiles_r[:, prev, :], SLOT_TILES), ramp_over, ALU.is_le))
                link(dve.tensor_reduce(expert_f, cv, AX.X, ALU.add))
                dve.tensor_scalar(expert_i, expert_f, float(E - 1), None, ALU.min)
                link(dve.tensor_tensor(cv, cv, over_tiles(tiles_r[:, 0, :], SLOT_TILES), ALU.mult))
                link(dve.tensor_reduce(start_r, cv, AX.X, ALU.add))
                link(dve.tensor_tensor(start_r, ramp_tile, start_r, ALU.subtract))
                link(dve.tensor_scalar(start_r, start_r, float(P), None, ALU.mult))
                dve.scalar_tensor_tensor(out=row_i, in0=expert_f, scalar=float(REGION), in1=start_r,
                                         op0=ALU.mult, op1=ALU.add).then_inc(table_ready, 1)

            dve.wait_ge(gates_ready, 1)
            dve.wait_ge(ramp_ready, RAMPS)
            split_scores(0)
            make_mask(0)
            mask_max(0)
            mask_max(1)
            for w in range(ALL_UNITS):
                L, u = w // UNITS, w % UNITS
                filled, pieces = fill_pieces(w)
                if L in TIGHT and u == 2:
                    for piece in pieces:
                        shared_piece(filled, piece, 0)
                    pieces = ()
                early = pieces and L in TIGHT and u == 1
                if early:
                    shared_piece(filled, pieces[0], 0)
                if w + 2 < ALL_UNITS:
                    mask_max(w + 2)
                if w == 0:
                    make_mask(1)
                if w == UNITS * 2 + 3:
                    make_mask(3)
                if u == 0 and 0 < L < STREAM - 1 and L not in TIGHT:
                    split_scores(L + 1)
                if pieces and pieces[0] < PIECES and not early:
                    shared_piece(filled, pieces[0], 0)
                if u == 0 and L >= 1:
                    divide(L - 1)
                if pieces and pieces[0] < PIECES:
                    shared_piece(filled, pieces[1], 0)
                if u == (0 if L in TIGHT else 1) and L >= 1:
                    end_elu(L - 1)
                if u == 1 and (L == 0 or L in TIGHT):
                    split_scores(L + 1)
                if u == 1 and L >= 1 and ORDER[L - 1][1] == 1:
                    after_attention(ORDER[L - 1][0])
                if w == UNITS * 2 + 1:
                    make_mask(2)
                if w in ROUTE_AT:
                    choose(filled)
                if w - 1 in ROUTE_AT:
                    place(filled, ps_f)
                if w - (FILL_UNITS - 1) in FILL_AT:
                    save_base(filled, ps_gu.rearrange("p (h d) -> p h d", h=HV))
            divide(STREAM - 1)
            for n in range(PAIR, B):
                for i in range(PIECES):
                    shared_piece(n, i, (PIECES * (n - PAIR) + i) % 3)
                    if n == PAIR and i == 0:
                        end_elu(STREAM - 1)
                    if i == 3:
                        choose(n)
                    if n == PAIR and i == 5:
                        after_attention(B - 1)
                    if i == 7:
                        place(n, ps_o)
                if n == B - 1:
                    make_table()
                save_base(n, ps_y[:, :, n % PAIR, :])

            dve.wait_ge(st_base, 16 * B)

            def hidden_chunk(q, r, c):
                c0, cw = GATE_CHUNKS[c]
                silu_up(3 * (SLOTS_IN * q + r) + c, r_tanh, r_silu, r_hid, c, cw, ps_chunk[c][:, 0:cw],
                        ps_chunk[c][:, cw:2 * cw], hid[:, r % 2, c0:c0 + cw])

            def scale_output(q, r):
                j = SLOTS_IN * q + r
                dve.wait_ge(r_y, j + 1)
                if not isinstance(j, int) or j >= 2:
                    dve.wait_ge(r_add, 16 * (j - 1))
                dve.tensor_scalar(y_sb[:, r % 2, :], ps_o[:, 0:D], tile_in[:, r % SLOTS_IN, W_COL:W_COL + 1], None, ALU.mult
                                  ).then_inc(r_ysb, 1)

            def step(q, r):
                s = SLOTS_IN * q + r
                inner = not isinstance(s, int)
                if inner or s < SLOT_TILES:
                    hidden_chunk(q, r, 0)
                if inner or s >= 2:
                    scale_output(q, r - 2)
                if inner or s < SLOT_TILES:
                    hidden_chunk(q, r, 1)
                    hidden_chunk(q, r, 2)

            for s in range(PEELED):
                step(0, s)
            with dve.Fori(0, ROUTED_LOOPS) as q:
                for r in range(PEELED, PEELED + SLOTS_IN):
                    step(q, r)
            for s in range(PEELED + SLOTS_IN * ROUTED_LOOPS, SLOT_TILES + 2):
                step(0, s)


def kernel(x, ctx_512, g_xattn, g_ffn, L0_xattn_W0, L0_xattn_a_self0, L0_xattn_a_neigh0, L0_xattn_b0,
           L0_xattn_W1, L0_xattn_a_self1, L0_xattn_a_neigh1, L0_xattn_b1, L0_ffn_w_router, L0_ffn_wg,
           L0_ffn_wu, L0_ffn_wd, L0_ffn_sg, L0_ffn_su, L0_ffn_sd):
    import numpy as np
    import concourse.bacc as bacc
    from concourse import mybir
    from concourse.bass_utils import run_bass_kernel_spmd

    def expert_rows(gate, up, down):
        n = gate.shape[0]
        g = np.asarray(gate).transpose(0, 2, 1).reshape(n, KC, P, I)
        u = np.asarray(up).transpose(0, 2, 1).reshape(n, KC, P, I)
        cols = []
        for c0, cw in GATE_CHUNKS:
            cols += [g[..., c0:c0 + cw], u[..., c0:c0 + cw]]
        gu = np.concatenate(cols, -1).transpose(0, 2, 1, 3).reshape(n, P, KC * GU)
        d = np.asarray(down).transpose(0, 2, 1).reshape(n, IC, P, D).transpose(0, 2, 1, 3).reshape(n, P, IC * D)
        return np.concatenate([gu, d], -1)

    arrays = {
        "x": np.asarray(x).reshape(T, D),
        "ctx_t": np.asarray(ctx_512).transpose(0, 2, 1),
        "w0": np.asarray(L0_xattn_W0).transpose(1, 0, 2).reshape(F_IN, HEADS * FO),
        "w1": np.asarray(L0_xattn_W1).transpose(1, 0, 2).reshape(D, HEADS * FO),
        "params": np.concatenate([np.asarray(a).reshape(-1) for a in (
            L0_xattn_a_self0, L0_xattn_a_neigh0, L0_xattn_a_self1, L0_xattn_a_neigh1,
            L0_xattn_b0, L0_xattn_b1, g_xattn, g_ffn)]),
        "w_router": np.asarray(L0_ffn_w_router).transpose(1, 0),
        "w_experts": np.concatenate([expert_rows(L0_ffn_wg, L0_ffn_wu, L0_ffn_wd),
                                     expert_rows(L0_ffn_sg, L0_ffn_su, L0_ffn_sd)], 0),
    }
    arrays = {n: np.ascontiguousarray(a) for n, a in arrays.items()}
    nc = bacc.Bacc("TRN2", target_bir_lowering=False, num_devices=1)
    args = {n: nc.dram_tensor(n, a.shape, mybir.dt.from_np(a.dtype), kind="ExternalInput").ap()
            for n, a in arrays.items()}
    args["slots"] = nc.dram_tensor("slots", (REGIONS * REGION, ROW), mybir.dt.float32, kind="Internal").ap()
    args["out"] = nc.dram_tensor("out", (T + P, D), mybir.dt.float32, kind="ExternalOutput").ap()
    build(nc, **args)
    r = run_bass_kernel_spmd(nc, [arrays], core_ids=[0])
    return r.results[0]["out"][0:T].reshape(B, N, D)
```
